# Optimizing a Trainium2 kernel written in Bass

```python
import numpy as np
import jax
import jax.numpy as jnp

def _softmax(x, axis=-1):
    return jax.nn.softmax(x, axis=axis)

def _gelu(x):
    return jax.nn.gelu(x, approximate=True)

def _silu(x):
    return jax.nn.silu(x)

def _sigmoid(x):
    return jax.nn.sigmoid(x)

def _layernorm(x, axis=-1, eps=1e-05):
    m = jnp.mean(x, axis=axis, keepdims=True)
    v = jnp.var(x, axis=axis, keepdims=True)
    return (x - m) / jnp.sqrt(v + eps)

def _scatter_add(tgt, idx, src, axis=0):
    return tgt.at[idx].add(src)

def _segment_sum(src, seg, n):
    return jax.ops.segment_sum(src, seg, n)
kernel_name = 'mk_prb_d1_jaxref_r8_f38f38'

def setup_inputs(seed: int=0):
    np.random.seed(seed)
    _w = jnp.asarray

    def _L0_attn_setup():
        import jax, jax.numpy as jnp
        import numpy as np
        B, L, D, H = (4, 512, 256, 16)
        HD = D // H
        EPS = 1e-09

        def phi(x):
            return jax.nn.elu(x) + 1.0
        key = jax.random.key(seed)
        k1, k2, k3 = jax.random.split(key, 3)
        x = jax.random.normal(k1, (B, L, D), dtype=jnp.float32)
        W_qkv = jax.random.normal(k2, (3 * D, D), dtype=jnp.float32) * D ** (-0.5)
        W_out = jax.random.normal(k3, (D, D), dtype=jnp.float32) * D ** (-0.5)
        return {'x': x, 'W_qkv': W_qkv, 'W_out': W_out}
    _L0_attn_in = _L0_attn_setup()

    def _L0_ffn_setup():
        import jax, jax.numpy as jnp
        import numpy as np
        HID = 256
        E = 8
        TOP_K = 2
        F = 176
        FS = 352
        SCALE = 2.5
        key = jax.random.key(seed)
        ks = jax.random.split(key, 8)
        s = 0.02
        return {'hidden_states': jax.random.normal(ks[0], (1, 256, HID), jnp.float32), 'w_router': jax.random.normal(ks[1], (HID, E), jnp.float32) * s, 'w_gate': jax.random.normal(ks[2], (E, HID, F), jnp.float32) * s, 'w_up': jax.random.normal(ks[3], (E, HID, F), jnp.float32) * s, 'w_down': jax.random.normal(ks[4], (E, F, HID), jnp.float32) * s, 'ws_gate': jax.random.normal(ks[5], (HID, FS), jnp.float32) * s, 'ws_up': jax.random.normal(ks[6], (HID, FS), jnp.float32) * s, 'ws_down': jax.random.normal(ks[7], (FS, HID), jnp.float32) * s}
    _L0_ffn_in = _L0_ffn_setup()
    _d = {'L0_attn_x': _L0_attn_in['x'], 'L0_attn_W_qkv': _L0_attn_in['W_qkv'], 'L0_attn_W_out': _L0_attn_in['W_out'], 'L0_ffn_w_router': _L0_ffn_in['w_router'], 'L0_ffn_w_gate': _L0_ffn_in['w_gate'], 'L0_ffn_w_up': _L0_ffn_in['w_up'], 'L0_ffn_w_down': _L0_ffn_in['w_down'], 'L0_ffn_ws_gate': _L0_ffn_in['ws_gate'], 'L0_ffn_ws_up': _L0_ffn_in['ws_up'], 'L0_ffn_ws_down': _L0_ffn_in['ws_down']}
    _x0 = _d['L0_attn_x']
    _d['L0_attn_x'] = jax.random.normal(jax.random.fold_in(jax.random.key(seed), 1), (4, 512, 256), dtype=_x0.dtype)
    del _x0
    return _d

def reference(L0_attn_x, L0_attn_W_qkv, L0_attn_W_out, L0_ffn_w_router, L0_ffn_w_gate, L0_ffn_w_up, L0_ffn_w_down, L0_ffn_ws_gate, L0_ffn_ws_up, L0_ffn_ws_down):

    def _L0_attn_ref(x, W_qkv, W_out):
        import jax, jax.numpy as jnp
        import numpy as np
        B, L, D, H = (4, 512, 256, 16)
        HD = D // H
        EPS = 1e-09

        def phi(x):
            return jax.nn.elu(x) + 1.0
        b, l, d = x.shape
        qkv = x @ W_qkv.T
        q, k, v = jnp.split(qkv, 3, axis=-1)
        q = q.reshape(b, l, H, HD).transpose(0, 2, 1, 3)
        k = k.reshape(b, l, H, HD).transpose(0, 2, 1, 3)
        v = v.reshape(b, l, H, HD).transpose(0, 2, 1, 3)
        q = phi(q)
        k = phi(k)
        kv_cumsum = jnp.cumsum(k * v, axis=2)
        k_cumsum = jnp.cumsum(k, axis=2)
        out = q * kv_cumsum / (q * k_cumsum + EPS)
        out = out.transpose(0, 2, 1, 3).reshape(b, l, d)
        return out @ W_out.T * HD ** (-0.5)

    def _L0_ffn_ref(hidden_states, w_router, w_gate, w_up, w_down, ws_gate, ws_up, ws_down):
        import jax, jax.numpy as jnp
        import numpy as np
        HID = 256
        E = 8
        TOP_K = 2
        F = 176
        FS = 352
        SCALE = 2.5
        B, S, D = hidden_states.shape
        x = hidden_states.reshape(-1, D)
        T = x.shape[0]
        probs = jax.nn.softmax(x @ w_router, axis=-1)
        top_v, top_i = jax.lax.top_k(probs, TOP_K)
        top_v = top_v / jnp.sum(top_v, axis=-1, keepdims=True)
        combine = jnp.zeros((T, E), x.dtype).at[jnp.arange(T)[:, None], top_i].set(top_v)
        g = jax.nn.silu(jnp.einsum('td,edf->etf', x, w_gate))
        u = jnp.einsum('td,edf->etf', x, w_up)
        y = jnp.einsum('etf,efd->etd', g * u, w_down)
        routed = jnp.einsum('etd,te->td', y, combine) * SCALE
        shared = jax.nn.silu(x @ ws_gate) * (x @ ws_up) @ ws_down
        return (routed + shared).reshape(B, S, D)
    x = L0_attn_x
    xn = _layernorm(x, axis=-1)
    x = x + _L0_attn_ref(xn, L0_attn_W_qkv, L0_attn_W_out) + _L0_ffn_ref(xn, L0_ffn_w_router, L0_ffn_w_gate, L0_ffn_w_up, L0_ffn_w_down, L0_ffn_ws_gate, L0_ffn_ws_up, L0_ffn_ws_down)
    return x

_drawn_inputs = setup_inputs


def setup_inputs(seed=0):
    import zlib

    import numpy as np

    out = dict(_drawn_inputs(seed))
    spreads = {}
    factors = {'L0_ffn_ws_gate': 2.882,
     'L0_ffn_ws_up': 2.852,
     'L0_ffn_ws_down': 2.846,
     'L0_ffn_w_router': 8.432}
    for name, (base, spread) in spreads.items():
        noise = np.random.default_rng([zlib.crc32(name.encode()), seed]).standard_normal(out[name].shape)
        drawn = base * np.exp(spread * noise) if base else spread * noise
        out[name] = jnp.asarray(drawn.astype(out[name].dtype))
    for name, factor in factors.items():
        out[name] = (out[name] * factor).astype(out[name].dtype)
    return out
```

```python
from contextlib import ExitStack

import concourse.bass as bass
from concourse import mybir

F32 = mybir.dt.float32
F32R = mybir.dt.float32r
F16 = mybir.dt.float16
I32 = mybir.dt.int32
ALU = mybir.AluOpType
ACT = mybir.ActivationFunctionType
AX = mybir.AxisListType.X

P = 128
T = 2048
D = 256
KD = D // P
NT = T // P
GT = 512
NG = T // GT
TG = GT // P
E = 8
F = 176
FH = F // 2
FS = 352
SCH = [(0, 128), (128, 128), (256, 96)]
NS = 40
SCALE = 2.5
HD_SCALE = 0.25
EPS_LN = 1e-5
EPS_ATT = 1e-9

C_ID, C_TRI, C_DESC, C_RESET, C_THR, C_I40, C_I128, C_TOK, C_END = (
    0, 128, 256, 264, 392, 408, 448, 576, 608)

W_OUT = KD * 3 * D
W_SDN = KD * 2 * FS
W_COLS = W_SDN + 3 * D
EG = KD * 2 * F
ED = 2 * D

B_K, B_V, B_Q, B_PROJ, B_ROUTE = 0, 1, 2, 6, 7
L_OFF, R_OFF, T_OFF, TAB_OFF = 0, 128, 256, 384

(W_EQ, W_EK, W_RQ, W_RK, W_NUM, W_P, W_KC, W_KVC, W_SLOTS) = (0, 1, 2, 4, 6, 8, 10, 12, 14)


UNITS = 2 * NG
CHUNKS = 3 * NG
WD = (0, W_OUT, W_OUT + KD * D)
WS = (0, W_SDN, W_SDN + 2 * D, W_COLS)
WS_ROWS = (P, P, SCH[2][1])


def wait_if(eng, s, n):
    if not (isinstance(n, int) and n <= 0):
        eng.wait_ge(s, n)


def build(nc, x, consts, wr, wqkv, wout, wsgu, wsdn_a, wsdn_b, egu, edn, out):
    xn_dram = nc.dram_tensor("xn_rows", (T, D), F32).ap()
    y_dram = nc.dram_tensor("y_rows", (NS * P, D), F32).ap()

    with ExitStack() as ctx:
        def sb(name, shape, dt):
            return ctx.enter_context(nc.sbuf_tensor(name, shape, dt))

        def sem(name):
            return ctx.enter_context(nc.semaphore(name))

        ps = ctx.enter_context(nc.psum_tensor("ps", [P, 8, 512], F32))
        x_acc = sb("x_acc", [P, NT, D], F32)
        xT_hi = sb("xT_hi", [P, KD, T], F32R)
        xT_lo = sb("xT_lo", [P, KD, T], F32R)
        w_hi = sb("w_hi", [P, W_COLS], F32R)
        w_lo = sb("w_lo", [P, W_COLS], F32R)
        wr_raw = sb("wr_raw", [P, KD * E], F32)
        wr_hi = sb("wr_hi", [P, KD * E], F32R)
        wr_lo = sb("wr_lo", [P, KD * E], F32R)
        eg_hi = sb("eg_hi", [P, E * EG], F32R)
        eg_lo = sb("eg_lo", [P, E * EG], F32R)
        ed_hi = sb("ed_hi", [FH, E * ED], F32R)
        ed_lo = sb("ed_lo", [FH, E * ED], F32R)
        e_raw = sb("e_raw", [P, EG + ED], F32)
        t_hi = sb("t_hi", [P, 4, GT], F32R)
        t_lo = sb("t_lo", [P, 4, GT], F32R)
        work = sb("work", [P, W_SLOTS, GT], F32)
        xg = sb("xg", [P, 4, D], F32)
        cst = sb("cst", [P, C_END], F32)
        ones = sb("ones", [P, P], F32)
        stats = sb("stats", [P, TG, 6], F32)
        mv = sb("mv", [P, NT, 2], F32)
        std = sb("std", [P, NT], F32)
        rz = sb("rz", [P, NT, E], F32)
        rp = sb("rp", [P, NT, E], F32)
        rc = sb("rc", [P, NT, E], F32)
        m1 = sb("m1", [P, NT, E], F32)
        m2 = sb("m2", [P, NT, E], F32)
        small = sb("small", [P, 8, NT], F32)
        wgt = sb("wgt", [P, 2, NT], F32)
        tot = sb("tot", [P, E, NT], F32)
        etab_w = sb("etab_w", [1, NS, E], F32)
        pm_i = sb("pm_i", [P, 2 * NT], I32)
        eps_col = sb("eps_col", [P, 1], F32)
        slot = sb("slot", [P, 2 * NT], F32)
        slot_i = sb("slot_i", [P, 2 * NT], I32)
        pm = sb("pm", [P, 2 * NT], F32)
        jm = sb("jm", [P, 2 * NT], F32)
        hotj = sb("hotj", [P, 2 * NT, NS], F16)
        tok_i = sb("tok_i", [P, NS], I32)
        etab_f = sb("etab_f", [1, NS], F32)
        etab = sb("etab", [1, NS], I32)

        x_in = [sem(f"x_in{g}") for g in range(NG)]
        cst_in, wr_in, wd_in, ws_in, e_in = (sem(n) for n in ("cst_in", "wr_in", "wd_in", "ws_in", "e_in"))
        xn_out, acc_out = sem("xn_out"), sem("acc_out")
        stat_s, var_ready, std_ready, rstd_ready, xn_ready = (
            sem(n) for n in ("stat_s", "var_ready", "std_ready", "rstd_ready", "xn_ready"))
        tr_ready, xT_hi_ready, xT_lo_ready, logits_ready = (
            sem(n) for n in ("tr_ready", "xT_hi_ready", "xT_lo_ready", "logits_ready"))
        ones_ready, wr_hi_s, wr_lo_s = sem("ones_ready"), sem("wr_hi_s"), sem("wr_lo_s")
        wd_hi_s, wd_lo_s, ws_hi_s, ws_lo_s, e_hi_s, e_lo_s = (
            sem(n) for n in ("wd_hi_s", "wd_lo_s", "ws_hi_s", "ws_lo_s", "e_hi_s", "e_lo_s"))
        k_ready, v_ready, q_ready, k_act, q_act = (
            sem(n) for n in ("k_ready", "v_ready", "q_ready", "k_act", "q_act"))
        phik_s, kv_s, kc_s, kvc_s, phiq_s = (sem(n) for n in ("phik_s", "kv_s", "kc_s", "kvc_s", "phiq_s"))
        den_s, num_s, ln_s, rec_s, out_s, o_hi, o_lo = (
            sem(n) for n in ("den_s", "num_s", "ln_s", "rec_s", "out_s", "o_hi", "o_lo"))
        proj_ready, acc_done = sem("proj_ready"), sem("acc_done")
        rt, z_ready, ez_ready, mask_ready, prefix_ready = (
            sem(n) for n in ("rt", "z_ready", "ez_ready", "mask_ready", "prefix_ready"))
        hot_ready, hot_used, tab_ready, tok_ready, etab_ready, slots_ready = (
            sem(n) for n in ("hot_ready", "hot_used", "tab_ready", "tok_ready", "etab_ready", "slots_ready"))
        gathered = [sem(f"gathered{b}") for b in range(4)]
        xt_ready, xt_hi_s, xt_lo_s, gu_ready, silu_s, h_s = (
            sem(n) for n in ("xt_ready", "xt_hi_s", "xt_lo_s", "gu_ready", "silu_s", "h_s"))
        ht_ready, ht_hi_s, ht_lo_s, y_ready, y_copied = (
            sem(n) for n in ("ht_ready", "ht_hi_s", "ht_lo_s", "y_ready", "y_copied"))
        y_stored = [sem(f"y_stored{b}") for b in range(2)]
        g_ready, u_ready, s_silu, s_h, s_hi, s_lo, down_ready = (
            sem(n) for n in ("g_ready", "u_ready", "s_silu", "s_h", "s_hi", "s_lo", "down_ready"))
        y_in = [sem(f"y_in{b}") for b in range(4)]
        add1, add2, fin_s = sem("add1"), sem("add2"), sem("fin_s")

        def flat(i, n=1):
            return work[:, i:i + n, :].rearrange("p a b -> p (a b)")

        wd_raw = flat(W_NUM, 4)
        ws_raw = flat(0, 5)[:, 0:W_COLS]
        xn_rows = flat(W_KC, 4).rearrange("p (i d) -> p i d", d=D)

        s_buf = work[:, 6, 0:2 * F].rearrange("p (b f) -> p b f", b=2)
        h_buf = work[:, 7, 0:2 * F].rearrange("p (b f) -> p b f", b=2)
        y_buf = work[:, 8, :].rearrange("p (b f) -> p b f", b=2)

        def xt(t, b):
            return t[:, 0, b * D:(b + 1) * D]

        def ht(t, b):
            return t[0:FH, 1, b * D:(b + 1) * D]

        yg = flat(10, 2).rearrange("p (b d) -> p b d", b=4)

        block = ctx.enter_context(nc.Block())

        @block.sync
        def _(sp):
            xv = x.rearrange("(t p) d -> p t d", p=P)
            ov = out.rearrange("(t p) d -> p t d", p=P)
            nv = xn_dram.rearrange("(t p) d -> p t d", p=P)
            yv = y_dram.rearrange("(t p) d -> p t d", p=P)

            sp.dma_start(x_acc[:, 0:TG, :], xv[:, 0:TG, :]).then_inc(x_in[0], 16)
            sp.dma_start(cst[:], consts).then_inc(cst_in, 16)
            sp.dma_start(wr_raw[:], wr).then_inc(wr_in, 16)
            for g in range(1, NG):
                sp.dma_start(x_acc[:, g * TG:(g + 1) * TG, :],
                             xv[:, g * TG:(g + 1) * TG, :]).then_inc(x_in[g], 16)
            sp.dma_start(wd_raw[:, 0:W_OUT], wqkv).then_inc(wd_in, 16)
            sp.dma_start(wd_raw[:, W_OUT:W_OUT + KD * D], wout).then_inc(wd_in, 16)
            for g in range(NG):
                sp.wait_ge(xn_ready, TG * (g + 1))
                sp.dma_start(nv[:, g * TG:(g + 1) * TG, :],
                             xn_rows[:, TG * (g % 2):TG * (g % 2 + 1), :]).then_inc(xn_out, 16)
                if g < NG - 1:
                    sp.wait_ge(xn_out, 16 * (g + 1))
            for e in range(E):
                if e:
                    sp.wait_ge(e_hi_s, 2 * e)
                    sp.wait_ge(e_lo_s, 2 * e)
                sp.dma_start(e_raw[:, 0:EG], egu[:, e, :]).then_inc(e_in, 16)
                sp.dma_start(e_raw[0:FH, EG:EG + ED], edn[:, e, :]).then_inc(e_in, 16)
            sp.wait_ge(o_lo, 2 * NG)
            sp.dma_start(ws_raw[:, 0:W_SDN], wsgu).then_inc(ws_in, 16)
            sp.dma_start(ws_raw[:, W_SDN:W_SDN + 2 * D], wsdn_a).then_inc(ws_in, 16)
            sp.dma_start(ws_raw[0:SCH[2][1], W_SDN + 2 * D:W_COLS], wsdn_b).then_inc(ws_in, 16)
            with sp.Fori(0, NS // 2) as j:
                for b in range(2):
                    sp.wait_ge(y_copied, j * 2 + (b + 1))
                    sp.dma_start(yv[:, bass.ds(j * 2 + b, 1), :],
                                 y_buf[:, b:b + 1, :]).then_inc(y_stored[b], 16)
            for g in range(NG):
                for h in range(2):
                    sp.wait_ge(fin_s, 2 * g + h + 1)
                    a = TG * g + 2 * h
                    sp.dma_start(ov[:, a:a + 2, :], x_acc[:, a:a + 2, :]).then_inc(acc_out, 16)
            sp.wait_ge(acc_out, 16 * 2 * NG)
            sp.wait_ge(xn_out, 16 * NG)

        @block.gpsimd
        def _(pool):
            q = nc.gpsimd
            q.memset(ones[:], 1.0).then_inc(ones_ready, 1)
            q.memset(eps_col[:], EPS_ATT).then_inc(ones_ready, 1)

            def low(dst, raw, high, done):
                q.tensor_tensor(dst, raw, high.bitcast(F32), ALU.subtract).then_inc(done, 1)

            pool.wait_ge(wr_hi_s, 1)
            low(wr_lo[:], wr_raw[:], wr_hi[:], wr_lo_s)
            for h in range(2):
                pool.wait_ge(wd_hi_s, h + 1)
                low(w_lo[:, WD[h]:WD[h + 1]], wd_raw[:, WD[h]:WD[h + 1]], w_hi[:, WD[h]:WD[h + 1]], wd_lo_s)
            for u in range(UNITS):
                c = u % 2
                pool.wait_ge(e_hi_s, 2 * u + 2)
                low(eg_lo[:, u * EG:(u + 1) * EG], e_raw[:, 0:EG], eg_hi[:, u * EG:(u + 1) * EG], e_lo_s)
                low(ed_lo[:, u * ED:(u + 1) * ED], e_raw[0:FH, EG:EG + ED], ed_hi[:, u * ED:(u + 1) * ED], e_lo_s)
                pool.wait_ge(phiq_s, u + 1)
                pool.wait_ge(kc_s, u + 1)
                if u >= 2:
                    pool.wait_ge(out_s, u - 1)
                q.tensor_tensor(work[:, W_P + c, :], work[:, W_RQ + c, :], work[:, W_KC + c, :],
                                ALU.mult).then_inc(den_s, 1)
                pool.wait_ge(kvc_s, u + 1)
                if u >= 2:
                    pool.wait_ge(o_lo, u - 1)
                q.tensor_tensor(work[:, W_NUM + c, :], work[:, W_RQ + c, :], work[:, W_KVC + c, :],
                                ALU.mult).then_inc(num_s, 1)

            pool.wait_ge(tok_ready, 1)
            pool.wait_ge(xn_out, 16 * NG)

            def gather(t):
                q.indirect_dma_start(
                    out=xg[:, t % 4, :], out_offset=None, in_=xn_dram,
                    in_offset=bass.IndirectOffsetOnAxis(ap=tok_i[:, t:t + 1], axis=0),
                ).then_inc(gathered[t % 4], 16)

            for t in range(4):
                gather(t)
            for h in range(3):
                n = WS_ROWS[h]
                pool.wait_ge(ws_hi_s, h + 1)
                low(w_lo[0:n, WS[h]:WS[h + 1]], ws_raw[0:n, WS[h]:WS[h + 1]], w_hi[0:n, WS[h]:WS[h + 1]], ws_lo_s)
            for t in range(4, NS):
                pool.wait_ge(xt_ready, t - 3)
                gather(t)

            for b in range(2):
                pool.wait_ge(y_stored[b], 16 * (NS // 2))
            for i in range(NT):
                for k in range(2):
                    b = (2 * i + k) % 4
                    if i >= 2:
                        pool.wait_ge((add1, add2)[k], i - 1)
                    q.indirect_dma_start(
                        out=yg[:, b, :], out_offset=None, in_=y_dram,
                        in_offset=bass.IndirectOffsetOnAxis(ap=slot_i[:, k * NT + i:k * NT + i + 1], axis=0),
                    ).then_inc(y_in[b], 16)

        @block.scalar
        def _(act):
            a = nc.scalar

            def high(dst, raw, done):
                a.activation(dst, raw, ACT.Copy).then_inc(done, 1)

            def sqrt(g):
                act.wait_ge(var_ready, g + 1)
                a.activation(std[:, g * TG:(g + 1) * TG], mv[:, g * TG:(g + 1) * TG, 1],
                             ACT.Sqrt).then_inc(std_ready, 1)

            def xT_high(g):
                for k in range(KD):
                    act.wait_ge(tr_ready, 2 * g + k + 1)
                    high(xT_hi[:, k, g * GT:(g + 1) * GT], ps[:, 2 + 2 * (g % 2) + k, :], xT_hi_ready)

            sqrt(0)
            sqrt(1)
            xT_high(0)
            sqrt(2)
            act.wait_ge(wr_in, 16)
            high(wr_hi[:], wr_raw[:], wr_hi_s)
            xT_high(1)
            sqrt(3)
            act.wait_ge(wd_in, 32)
            for h in range(2):
                high(w_hi[:, WD[h]:WD[h + 1]], wd_raw[:, WD[h]:WD[h + 1]], wd_hi_s)
            xT_high(2)
            xT_high(3)

            def expert_high(e):
                act.wait_ge(e_in, 32 * (e + 1))
                high(eg_hi[:, e * EG:(e + 1) * EG], e_raw[:, 0:EG], e_hi_s)
                high(ed_hi[:, e * ED:(e + 1) * ED], e_raw[0:FH, EG:EG + ED], e_hi_s)

            def k_parts(u):
                c, b = u % 2, 3 * (u % 2)
                act.wait_ge(k_ready, u + 1)
                if u >= 1:
                    act.wait_ge(kvc_s, u)
                a.activation(work[:, W_EK, :], ps[:, b + B_K, :], ACT.Exp)
                a.activation(work[:, W_RK + c, :], ps[:, b + B_K, :], ACT.Relu).then_inc(k_act, 1)

            def q_parts(u):
                c, b = u % 2, 3 * (u % 2)
                act.wait_ge(q_ready, u + 1)
                if u >= 1:
                    act.wait_ge(phiq_s, u)
                if u >= 2:
                    act.wait_ge(num_s, u - 1)
                a.activation(work[:, W_EQ, :], ps[:, b + B_Q, :], ACT.Exp)
                a.activation(work[:, W_RQ + c, :], ps[:, b + B_Q, :], ACT.Relu).then_inc(q_act, 1)

            def reciprocal(u):
                d = work[:, W_P + u % 2, :]
                act.wait_ge(den_s, u + 1)
                a.activation(d, d, ACT.Ln, bias=eps_col[:, 0:1]).then_inc(ln_s, 1)
                act.wait_ge(ln_s, u + 1)
                a.activation(d, d, ACT.Exp, scale=-1.0).then_inc(rec_s, 1)

            def out_high(u):
                act.wait_ge(out_s, u + 1)
                if u >= 4:
                    act.wait_ge(proj_ready, 2 * ((u - 4) // 2 + 1))
                high(t_hi[:, u % 4, :], work[:, W_NUM + u % 2, :], o_hi)

            act.wait_ge(ones_ready, 2)
            for u in range(UNITS + 2):
                if u < UNITS:
                    k_parts(u)
                if u >= 2:
                    out_high(u - 2)
                if u < UNITS:
                    q_parts(u)
                if u == 0:
                    act.wait_ge(z_ready, 1)
                    a.activation(rz[:], rz[:], ACT.Exp).then_inc(ez_ready, 1)
                if 1 <= u <= UNITS:
                    reciprocal(u - 1)
                if u < E:
                    expert_high(u)

            act.wait_ge(proj_ready, 2 * NG)
            act.wait_ge(ws_in, 48)
            for h in range(3):
                n = WS_ROWS[h]
                high(w_hi[0:n, WS[h]:WS[h + 1]], ws_raw[0:n, WS[h]:WS[h + 1]], ws_hi_s)

            def h_high(t, b):
                act.wait_ge(ht_ready, t + 1)
                wait_if(act, y_ready, t - 1)
                high(ht(t_hi, b), ps[0:FH, 4 + b, 0:D], ht_hi_s)

            def x_high(t, b):
                act.wait_ge(xt_ready, t + 1)
                wait_if(act, gu_ready, t - 1)
                high(xt(t_hi, b), ps[:, b, 0:D], xt_hi_s)

            def silu(t, b):
                act.wait_ge(gu_ready, t + 1)
                wait_if(act, h_s, t - 1)
                a.activation(s_buf[:, b, :], ps[:, 2 + b, 0:F], ACT.Silu).then_inc(silu_s, 1)

            def y_copy(t, b, stored):
                act.wait_ge(y_ready, t + 1)
                wait_if(act, y_stored[b], stored)
                a.activation(y_buf[:, b, :], ps[:, 6 + b, 0:D], ACT.Copy).then_inc(y_copied, 1)

            def r_step(j, b, first=False, last=False):
                t = j * 2 + b
                if not first:
                    h_high(t - 1, 1 - b)
                if not last:
                    x_high(t + 1, 1 - b)
                silu(t, b)
                if not first:
                    y_copy(t - 1, 1 - b, (j - 1) * 16 if b == 0 else j * 16)

            x_high(0, 0)
            r_step(0, 0, first=True)
            r_step(0, 1)
            with act.Fori(1, NS // 2 - 1) as j:
                for b in range(2):
                    r_step(j, b)
            r_step(NS // 2 - 1, 0)
            r_step(NS // 2 - 1, 1, last=True)
            h_high(NS - 1, 1)
            y_copy(NS - 1, 1, 16 * (NS // 2 - 1))

            def s_high(i):
                n = SCH[i % 3][1]
                act.wait_ge(s_h, i + 1)
                if i < 4:
                    act.wait_ge(y_ready, NS)
                else:
                    act.wait_ge(down_ready, 2 * ((i - 4) // 3 + 1))
                high(t_hi[0:n, i % 4, :], work[0:n, 2 + i % 2, :], s_hi)

            act.wait_ge(ws_lo_s, 3)
            for i in range(CHUNKS):
                n = SCH[i % 3][1]
                act.wait_ge(g_ready, i + 1)
                if i >= 2:
                    act.wait_ge(s_h, i - 1)
                a.activation(work[0:n, i % 2, :], ps[0:n, 2 * (i % 2), :], ACT.Silu).then_inc(s_silu, 1)
                if i >= 1:
                    s_high(i - 1)
            s_high(CHUNKS - 1)

        @block.vector
        def _(dve):
            v = nc.vector

            def low(dst, full, high, done):
                v.tensor_tensor(dst, full, high.bitcast(F32), ALU.subtract).then_inc(done, 1)

            def row_stats(g):
                dve.wait_ge(x_in[g], 16)
                if g:
                    dve.wait_ge(stat_s, 8 * g)
                for i in range(TG):
                    v.bn_stats(stats[:, i, :], x_acc[:, g * TG + i, :]).then_inc(stat_s, 1)
                dve.wait_ge(stat_s, 8 * g + 4)
                for i in range(TG):
                    v.bn_aggr(mv[:, g * TG + i, :], stats[:, i, :]).then_inc(stat_s, 1)
                dve.wait_ge(stat_s, 8 * g + 8)
                var = mv[:, g * TG:(g + 1) * TG, 1]
                v.tensor_scalar(var, var, EPS_LN, None, ALU.add).then_inc(var_ready, 1)

            def normed(g):
                dve.wait_ge(std_ready, g + 1)
                r = std[:, g * TG:(g + 1) * TG]
                v.reciprocal(r, r).then_inc(rstd_ready, 1)
                dve.wait_ge(rstd_ready, g + 1)
                if g >= 2:
                    dve.wait_ge(xn_out, 16 * (g - 1))
                    dve.wait_ge(tr_ready, 2 * (g - 1))
                for i in range(g * TG, (g + 1) * TG):
                    v.tensor_scalar(xn_rows[:, i % 8, :], x_acc[:, i, :], mv[:, i, 0:1], std[:, i:i + 1],
                                    ALU.subtract, ALU.mult).then_inc(xn_ready, 1)

            def xT_low(g):
                for k in range(KD):
                    dve.wait_ge(xT_hi_ready, 2 * g + k + 1)
                    cols = slice(g * GT, (g + 1) * GT)
                    low(xT_lo[:, k, cols], ps[:, 2 + 2 * (g % 2) + k, :], xT_hi[:, k, cols], xT_lo_ready)

            row_stats(0)
            row_stats(1)
            normed(0)
            row_stats(2)
            normed(1)
            xT_low(0)
            row_stats(3)
            normed(2)
            xT_low(1)
            normed(3)
            xT_low(2)
            xT_low(3)

            n_rt = [0]

            def link(ins):
                n_rt[0] += 1
                ins.then_inc(rt, 1)
                dve.wait_ge(rt, n_rt[0])

            def over_e(ap):
                return ap.unsqueeze(2).broadcast_to([P, NT, E])

            logits = ps[:, B_ROUTE, L_OFF:L_OFF + NT * E].rearrange("p (t e) -> p t e", e=E)
            desc = cst[:, C_DESC:C_DESC + E].unsqueeze(1).broadcast_to([P, NT, E])
            mx, sm, p1, p2, c1, ws = (small[:, n, :] for n in range(6))

            def route_logits():
                dve.wait_ge(logits_ready, 1)
                link(v.tensor_reduce(mx, logits, AX, ALU.max))
                v.tensor_tensor(rz[:], logits, over_e(mx), ALU.subtract).then_inc(z_ready, 1)

            def first_max(mask, top):
                link(v.tensor_reduce(top, rp[:], AX, ALU.max))
                link(v.tensor_tensor(rc[:], rp[:], over_e(top), ALU.is_equal))
                link(v.tensor_tensor(rc[:], rc[:], desc, ALU.mult))
                link(v.tensor_reduce(c1, rc[:], AX, ALU.max))
                link(v.tensor_tensor(mask, rc[:], over_e(c1), ALU.is_equal))

            def route_top2():
                dve.wait_ge(ez_ready, 1)
                link(v.tensor_reduce(sm, rz[:], AX, ALU.add))
                link(v.reciprocal(sm, sm))
                link(v.tensor_tensor(rp[:], rz[:], over_e(sm), ALU.mult))
                dve.wait_ge(cst_in, 16)
                first_max(m1[:], p1)
                link(v.scalar_tensor_tensor(out=rp[:], in0=m1[:], scalar=-2.0, in1=rp[:],
                                            op0=ALU.mult, op1=ALU.add))
                first_max(m2[:], p2)
                v.tensor_tensor(rz[:], m1[:], m2[:], ALU.add).then_inc(mask_ready, 1)
                link(v.tensor_tensor(ws, p1, p2, ALU.add))
                link(v.reciprocal(ws, ws))
                for k, pk in enumerate((p1, p2)):
                    link(v.scalar_tensor_tensor(out=wgt[:, k, :], in0=pk, scalar=SCALE, in1=ws,
                                                op0=ALU.mult, op1=ALU.mult))

            def route_slots():
                et = rc[:].rearrange("p t e -> p (t e)").rearrange("p (e t) -> p e t", e=E)
                cum = rp[:].rearrange("p t e -> p (t e)").rearrange("p (e t) -> p e t", e=E)
                one = ones[:, 0:E]
                dve.wait_ge(prefix_ready, 1)
                link(v.tensor_copy(et, ps[:, B_ROUTE, T_OFF:T_OFF + NT * E].rearrange("p (t e) -> p e t", e=E)))
                link(v.tensor_tensor_scan(rp[:].rearrange("p t e -> p (t e)"), cst[:, C_RESET:C_RESET + NT * E],
                                          rc[:].rearrange("p t e -> p (t e)"), 0.0, ALU.mult, ALU.add))
                thr = cst[:, C_THR:C_THR + NT].unsqueeze(1).broadcast_to([P, E, NT])
                link(v.tensor_tensor(tot[:, :, 0:NT], cum[:, :, NT - 1:NT].broadcast_to([P, E, NT]), thr, ALU.is_gt))
                link(v.tensor_reduce(small[:, 6, 0:E], tot[:, :, 0:NT], AX, ALU.add))
                dve.wait_ge(ones_ready, 2)
                link(v.tensor_tensor_scan(small[:, 6, E:2 * E], one, small[:, 6, 0:E], 0.0, ALU.mult, ALU.add))
                link(v.tensor_tensor(small[:, 7, 0:E], small[:, 6, E:2 * E], small[:, 6, 0:E], ALU.subtract))
                link(v.tensor_scalar(small[:, 7, 0:E], small[:, 7, 0:E], float(P), None, ALU.mult))
                link(v.tensor_tensor(rp[:].rearrange("p t e -> p (t e)"), rp[:].rearrange("p t e -> p (t e)"),
                                     rc[:].rearrange("p t e -> p (t e)"), ALU.subtract))
                link(v.tensor_tensor(cum, cum, small[:, 7, 0:E].unsqueeze(2).broadcast_to([P, E, NT]), ALU.add))
                before = ps[:, B_ROUTE, R_OFF:R_OFF + NT * E].rearrange("p (t e) -> p t e", e=E)
                link(v.tensor_tensor(rc[:], before, cum.rearrange("p e t -> p t e"), ALU.add))
                for k, m in enumerate((m1, m2)):
                    link(v.tensor_tensor(m[:], m[:], rc[:], ALU.mult))
                    link(v.tensor_reduce(slot[:, k * NT:(k + 1) * NT], m[:], AX, ALU.add))
                v.tensor_copy(slot_i[:], slot[:]).then_inc(slots_ready, 1)
                dve.wait_ge(slots_ready, 1)
                link(v.tensor_scalar(pm_i[:], slot_i[:], P - 1, None, ALU.bitwise_and))
                link(v.tensor_copy(pm[:], pm_i[:]))
                link(v.tensor_tensor(jm[:], slot[:], pm[:], ALU.subtract))
                link(v.tensor_scalar(jm[:], jm[:], 1.0 / P, None, ALU.mult))
                j40 = cst[0:1, C_I40:C_I40 + NS].unsqueeze(2).broadcast_to([1, NS, E])
                ends = small[0:1, 6, E:2 * E].unsqueeze(1).broadcast_to([1, NS, E])
                link(v.tensor_tensor(etab_w[:], j40, ends, ALU.is_ge))
                link(v.tensor_reduce(etab_f[:], etab_w[:], AX, ALU.add))
                v.tensor_scalar(etab[:], etab_f[:], float(E - 1), None, ALU.min).then_inc(etab_ready, 1)

            hotp = xg[:].rearrange("p b d -> p (b d)").bitcast(F16).rearrange("p (i s) -> p i s", s=P)

            def route_hot(k):
                if k == 0:
                    i40 = cst[:, C_I40:C_I40 + NS].unsqueeze(1).broadcast_to([P, 2 * NT, NS])
                    link(v.tensor_tensor(hotj[:], jm[:].unsqueeze(2).broadcast_to([P, 2 * NT, NS]), i40, ALU.is_equal))
                    tok = cst[:, C_TOK:C_TOK + 2 * NT].unsqueeze(2).broadcast_to([P, 2 * NT, NS])
                    link(v.tensor_tensor(hotj[:], hotj[:], tok, ALU.mult))
                else:
                    dve.wait_ge(hot_used, 1)
                i128 = cst[:, C_I128:C_I128 + P].unsqueeze(1).broadcast_to([P, NT, P])
                v.tensor_tensor(hotp, pm[:, k * NT:(k + 1) * NT].unsqueeze(2).broadcast_to([P, NT, P]), i128,
                                ALU.is_equal).then_inc(hot_ready, 1)

            def route_table():
                dve.wait_ge(hot_used, 2)
                v.tensor_copy(tok_i[:], ps[:, B_ROUTE, TAB_OFF:TAB_OFF + NS]).then_inc(tok_ready, 1)

            def keys(u):
                c, b = u % 2, 3 * (u % 2)
                ek, rk = work[:, W_EK, :], work[:, W_RK + c, :]
                kc, kvc = work[:, W_KC + c, :], work[:, W_KVC + c, :]
                dve.wait_ge(k_act, u + 1)
                v.scalar_tensor_tensor(out=rk, in0=ek, scalar=1.0, in1=rk, op0=ALU.min,
                                       op1=ALU.add).then_inc(phik_s, 1)
                dve.wait_ge(phik_s, u + 1)
                dve.wait_ge(v_ready, u + 1)
                v.tensor_tensor(ek, rk, ps[:, b + B_V, :], ALU.mult).then_inc(kv_s, 1)
                if u >= 2:
                    dve.wait_ge(den_s, u - 1)
                else:
                    dve.wait_ge(xn_out, 16 * NG)
                one = ones[:, 0:1].broadcast_to([P, GT])
                v.tensor_tensor_scan(kc, one, rk, 0.0, ALU.mult,
                                     ALU.add).then_inc(kc_s, 1)
                dve.wait_ge(kv_s, u + 1)
                if u >= 2:
                    dve.wait_ge(num_s, u - 1)
                v.tensor_tensor_scan(kvc, one, ek, 0.0, ALU.mult,
                                     ALU.add).then_inc(kvc_s, 1)

            def queries(u):
                c = u % 2
                rq = work[:, W_RQ + c, :]
                dve.wait_ge(q_act, u + 1)
                v.scalar_tensor_tensor(out=rq, in0=work[:, W_EQ, :], scalar=1.0, in1=rq, op0=ALU.min,
                                       op1=ALU.add).then_inc(phiq_s, 1)

            def divided(u):
                n = work[:, W_NUM + u % 2, :]
                dve.wait_ge(rec_s, u + 1)
                dve.wait_ge(num_s, u + 1)
                v.tensor_tensor(n, n, work[:, W_P + u % 2, :], ALU.mult).then_inc(out_s, 1)

            def out_low(u):
                dve.wait_ge(o_hi, u + 1)
                low(t_lo[:, u % 4, :], work[:, W_NUM + u % 2, :], t_hi[:, u % 4, :], o_lo)

            def add_proj(n):
                dve.wait_ge(proj_ready, n + 1)
                two = x_acc[:, 2 * n:2 * n + 2, :].rearrange("p a b -> p (a b)")
                v.scalar_tensor_tensor(out=two, in0=ps[:, B_PROJ, :], scalar=HD_SCALE, in1=two, op0=ALU.mult,
                                       op1=ALU.add).then_inc(acc_done, 1)

            route_logits()
            dve.wait_ge(ones_ready, 2)
            for u in range(UNITS + 2):
                if u < UNITS:
                    keys(u)
                    queries(u)
                if u >= 2:
                    out_low(u - 2)
                if 1 <= u <= UNITS:
                    divided(u - 1)
                if u == 0:
                    route_top2()
                if u == 2:
                    route_slots()
                if u == 3:
                    route_hot(0)
                if u == 4:
                    route_hot(1)
                if u == 5:
                    route_table()
                if 4 <= u <= 7:
                    add_proj(u - 4)
            for n in range(4, 2 * NG):
                add_proj(n)

            def h_low(t, b):
                dve.wait_ge(ht_hi_s, t + 1)
                low(ht(t_lo, b), ps[0:FH, 4 + b, 0:D], ht(t_hi, b), ht_lo_s)

            def x_low(t, b):
                dve.wait_ge(xt_hi_s, t + 1)
                low(xt(t_lo, b), ps[:, b, 0:D], xt(t_hi, b), xt_lo_s)

            def hidden(t, b):
                dve.wait_ge(silu_s, t + 1)
                wait_if(dve, ht_ready, t - 1)
                v.tensor_tensor(h_buf[:, b, :], s_buf[:, b, :], ps[:, 2 + b, F:2 * F], ALU.mult).then_inc(h_s, 1)

            def r_step(j, b, first=False, last=False):
                t = j * 2 + b
                if not first:
                    h_low(t - 1, 1 - b)
                if not last:
                    x_low(t + 1, 1 - b)
                hidden(t, b)

            x_low(0, 0)
            r_step(0, 0, first=True)
            r_step(0, 1)
            with dve.Fori(1, NS // 2 - 1) as j:
                for b in range(2):
                    r_step(j, b)
            r_step(NS // 2 - 1, 0)
            r_step(NS // 2 - 1, 1, last=True)
            h_low(NS - 1, 1)

            def s_hidden(i):
                n = SCH[i % 3][1]
                dve.wait_ge(s_silu, i + 1)
                dve.wait_ge(u_ready, i + 1)
                if i >= 2:
                    dve.wait_ge(s_lo, i - 1)
                v.tensor_tensor(work[0:n, 2 + i % 2, :], work[0:n, i % 2, :], ps[0:n, 2 * (i % 2) + 1, :],
                                ALU.mult).then_inc(s_h, 1)

            def s_low(i):
                n = SCH[i % 3][1]
                dve.wait_ge(s_hi, i + 1)
                low(t_lo[0:n, i % 4, :], work[0:n, 2 + i % 2, :], t_hi[0:n, i % 4, :], s_lo)

            def add_routed(i):
                for k in range(2):
                    b = (2 * i + k) % 4
                    dve.wait_ge(y_in[b], 16 * (i // 2 + 1))
                    if k:
                        dve.wait_ge(add1, i + 1)
                    v.scalar_tensor_tensor(out=x_acc[:, i, :], in0=yg[:, b, :], scalar=wgt[:, k, i:i + 1],
                                           in1=x_acc[:, i, :], op0=ALU.mult,
                                           op1=ALU.add).then_inc((add1, add2)[k], 1)

            def add_shared(n):
                dve.wait_ge(down_ready, n + 1)
                dve.wait_ge(add2, 2 * n + 2)
                two = x_acc[:, 2 * n:2 * n + 2, :].rearrange("p a b -> p (a b)")
                g, h = n // 2, n % 2
                v.tensor_tensor(two, two, ps[:, 4 + 2 * (g % 2) + h, :], ALU.add).then_inc(fin_s, 1)

            for i in range(CHUNKS + 1):
                if i < CHUNKS:
                    s_hidden(i)
                if i >= 1:
                    s_low(i - 1)
                if i % 3 == 0 and i:
                    g = i // 3 - 1
                    for t in range(g * TG, (g + 1) * TG):
                        add_routed(t)
                if i % 3 == 1 and i > 3:
                    g = i // 3 - 1
                    add_shared(2 * g)
                    add_shared(2 * g + 1)
            add_shared(2 * NG - 2)
            add_shared(2 * NG - 1)

        @block.tensor
        def _(pe):
            t_ = nc.tensor

            def three(out_ap, ws_, xs_, start, stop):
                t_.matmul(out_ap, ws_[0], xs_[0], start=start, stop=False)
                t_.matmul(out_ap, ws_[0], xs_[1], start=False, stop=False)
                return t_.matmul(out_ap, ws_[1], xs_[0], start=False, stop=stop)

            def rows_to_columns(g):
                for k in range(KD):
                    if g >= 2:
                        pe.wait_ge(xT_lo_ready, 2 * (g - 2) + k + 1)
                    for i in range(TG):
                        if k == 0:
                            pe.wait_ge(xn_ready, g * TG + i + 1)
                        mm = t_.transpose(ps[:, 2 + 2 * (g % 2) + k, i * P:(i + 1) * P],
                                          xn_rows[:, (g * TG + i) % 8, k * P:(k + 1) * P], cst[:, C_ID:C_ID + P])
                    mm.then_inc(tr_ready, 1)

            def logits(g):
                pe.wait_ge(xT_lo_ready, 2 * g + 2)
                for i in range(g * TG, (g + 1) * TG):
                    for k in range(KD):
                        cols = slice(i * P, (i + 1) * P)
                        e8 = slice(k * E, (k + 1) * E)
                        mm = three(ps[:, B_ROUTE, L_OFF + i * E:L_OFF + (i + 1) * E],
                                   (xT_hi[:, k, cols], xT_lo[:, k, cols]), (wr_hi[:, e8], wr_lo[:, e8]),
                                   k == 0, k == KD - 1)
                return mm

            pe.wait_ge(cst_in, 16)
            rows_to_columns(0)
            rows_to_columns(1)
            pe.wait_ge(wr_lo_s, 1)
            logits(0)
            rows_to_columns(2)
            logits(1)
            rows_to_columns(3)
            logits(2)
            logits(3).then_inc(logits_ready, 1)

            def qkv(u):
                g, c, b = u // 2, u % 2, 3 * (u % 2)
                cols = slice(g * GT, (g + 1) * GT)
                for bank, part, read, done in ((B_K, 2, k_act, k_ready), (B_V, 4, kv_s, v_ready),
                                               (B_Q, 0, q_act, q_ready)):
                    if u >= 2:
                        pe.wait_ge(read, u - 1)
                    for k in range(KD):
                        w = slice(k * 3 * D + (part + c) * P, k * 3 * D + (part + c + 1) * P)
                        mm = three(ps[:, b + bank, :], (w_hi[:, w], w_lo[:, w]),
                                   (xT_hi[:, k, cols], xT_lo[:, k, cols]), k == 0, k == KD - 1)
                    mm.then_inc(done, 1)

            def project(n):
                g = n // 2
                pe.wait_ge(o_lo, 2 * g + 2)
                if n:
                    pe.wait_ge(acc_done, n)
                for i in range(2):
                    cols = slice((2 * (n % 2) + i) * P, (2 * (n % 2) + i + 1) * P)
                    for c in range(KD):
                        s = (2 * g + c) % 4
                        w = slice(W_OUT + c * D, W_OUT + (c + 1) * D)
                        mm = three(ps[:, B_PROJ, i * D:(i + 1) * D], (t_hi[:, s, cols], t_lo[:, s, cols]),
                                   (w_hi[:, w], w_lo[:, w]), c == 0, c == KD - 1)
                mm.then_inc(proj_ready, 1)

            def prefix():
                pe.wait_ge(mask_ready, 1)
                pe.wait_ge(ones_ready, 2)
                mask = rz[:].rearrange("p t e -> p (t e)")
                t_.matmul(ps[:, B_ROUTE, R_OFF:R_OFF + NT * E], cst[:, C_TRI:C_TRI + P], mask, start=True, stop=True)
                t_.matmul(ps[:, B_ROUTE, T_OFF:T_OFF + NT * E], ones[:], mask, start=True,
                          stop=True).then_inc(prefix_ready, 1)

            def table(k):
                hotp = xg[:].rearrange("p b d -> p (b d)").bitcast(F16).rearrange("p (i s) -> p i s", s=P)
                pe.wait_ge(hot_ready, k + 1)
                for i in range(NT):
                    mm = t_.matmul(ps[:, B_ROUTE, TAB_OFF:TAB_OFF + NS], hotp[:, i, :], hotj[:, k * NT + i, :],
                                   start=(k == 0 and i == 0), stop=(k == 1 and i == NT - 1))
                mm.then_inc(hot_used, 1)

            pe.wait_ge(wd_lo_s, 2)
            pe.wait_ge(xT_lo_ready, 2 * NG)
            for u in range(UNITS):
                qkv(u)
                if u == 2:
                    prefix()
                if u == 4:
                    table(0)
                if u == 5:
                    table(1)
                if u >= 3 and u < 7:
                    project(u - 3)
            for n in range(4, 2 * NG):
                project(n)

            pe.wait_ge(etab_ready, 1)
            pe.wait_ge(e_lo_s, 2 * E)
            pe.wait_ge(acc_done, 2 * NG)
            pe.wait_ge(tok_ready, 1)

            def x_turn(t, b4, count):
                b = b4 % 2
                pe.wait_ge(gathered[b4], count)
                wait_if(pe, xt_lo_s, t - 1)
                for k in range(KD):
                    mm = t_.transpose(ps[:, b, k * P:(k + 1) * P], xg[:, b4, k * P:(k + 1) * P],
                                      cst[:, C_ID:C_ID + P])
                mm.then_inc(xt_ready, 1)

            def gate_up(t, b, e):
                pe.wait_ge(xt_lo_s, t + 1)
                wait_if(pe, h_s, t - 1)
                for k in range(KD):
                    w = bass.ds(e * EG + k * 2 * F, 2 * F)
                    xs = slice(b * D + k * P, b * D + (k + 1) * P)
                    mm = three(ps[:, 2 + b, 0:2 * F], (t_hi[:, 0, xs], t_lo[:, 0, xs]),
                               (eg_hi[:, w], eg_lo[:, w]), k == 0, k == KD - 1)
                mm.then_inc(gu_ready, 1)

            def h_turn(t, b):
                pe.wait_ge(h_s, t + 1)
                wait_if(pe, ht_lo_s, t - 1)
                for k in range(2):
                    mm = t_.transpose(ps[0:FH, 4 + b, k * P:(k + 1) * P], h_buf[:, b, k * FH:(k + 1) * FH],
                                      cst[:, C_ID:C_ID + P])
                mm.then_inc(ht_ready, 1)

            def down(t, b, e):
                pe.wait_ge(ht_lo_s, t + 1)
                wait_if(pe, y_copied, t - 1)
                for k in range(2):
                    w = bass.ds(e * ED + k * D, D)
                    hs = slice(b * D + k * P, b * D + (k + 1) * P)
                    mm = three(ps[:, 6 + b, 0:D], (t_hi[0:FH, 1, hs], t_lo[0:FH, 1, hs]),
                               (ed_hi[:, w], ed_lo[:, w]), k == 0, k == 1)
                mm.then_inc(y_ready, 1)

            def expert_of(t):
                return pe.value_load(etab[0:1, bass.ds(t, 1)], min_val=0, max_val=E - 1)

            def r_turn(j, first=False, last=False):
                for b in range(4):
                    t = j * 4 + b
                    if not (first and b == 0):
                        h_turn(t - 1, (b + 1) % 2)
                    if not (last and b == 3):
                        x_turn(t + 1, (b + 1) % 4, (j + 1) * 16 if b < 3 else (j + 2) * 16)
                    gate_up(t, b % 2, expert_of(t))
                    if not (first and b == 0):
                        down(t - 1, (b + 1) % 2, expert_of(t - 1))

            x_turn(0, 0, 16)
            r_turn(0, first=True)
            with pe.Fori(1, NS // 4 - 1) as j:
                r_turn(j)
            r_turn(NS // 4 - 1, last=True)
            h_turn(NS - 1, 1)
            down(NS - 1, 1, expert_of(NS - 1))

            def s_gate_up(i):
                g, (m0, n) = i // 3, SCH[i % 3]
                cols = slice(g * GT, (g + 1) * GT)
                for half, done in ((0, g_ready), (1, u_ready)):
                    if i >= 2:
                        pe.wait_ge((s_silu, s_h)[half], i - 1)
                    for k in range(KD):
                        w = slice(k * 2 * FS + half * FS + m0, k * 2 * FS + half * FS + m0 + n)
                        mm = three(ps[0:n, 2 * (i % 2) + half, :], (w_hi[:, w], w_lo[:, w]),
                                   (xT_hi[:, k, cols], xT_lo[:, k, cols]), k == 0, k == KD - 1)
                    mm.then_inc(done, 1)

            def s_down(g):
                pe.wait_ge(s_lo, 3 * g + 3)
                for h in range(2):
                    if g >= 2:
                        pe.wait_ge(fin_s, 2 * (g - 2) + h + 1)
                    for i in range(2):
                        cols = slice((2 * h + i) * P, (2 * h + i + 1) * P)
                        for m, (_, n) in enumerate(SCH):
                            s = (3 * g + m) % 4
                            w = slice(W_SDN + m * D, W_SDN + (m + 1) * D)
                            mm = three(ps[:, 4 + 2 * (g % 2) + h, i * D:(i + 1) * D],
                                       (t_hi[0:n, s, cols], t_lo[0:n, s, cols]),
                                       (w_hi[0:n, w], w_lo[0:n, w]), m == 0, m == 2)
                    mm.then_inc(down_ready, 1)

            pe.wait_ge(ws_lo_s, 3)
            pe.wait_ge(y_copied, NS)
            for i in range(CHUNKS):
                s_gate_up(i)
                if i % 3 == 0 and i:
                    s_down(i // 3 - 1)
            s_down(NG - 1)


def constants():
    import numpy as np
    c = np.zeros((P, C_END), np.float32)
    p = np.arange(P)
    c[:, C_ID:C_ID + P] = np.eye(P)
    c[:, C_TRI:C_TRI + P] = p[:, None] < p[None, :]
    c[:, C_DESC:C_DESC + E] = E - np.arange(E)
    c[:, C_RESET:C_RESET + E * NT] = (np.arange(E * NT) % NT) != 0
    c[:, C_THR:C_THR + NT] = P * np.arange(NT)
    c[:, C_I40:C_I40 + NS] = np.arange(NS)
    c[:, C_I128:C_I128 + P] = p
    c[:, C_TOK:C_TOK + 2 * NT] = p[:, None] + P * (np.arange(2 * NT) % NT)
    return c


def laid_out(a):
    import numpy as np

    def rows(w, k):
        return w.reshape(k, w.shape[0] // k, w.shape[1]).transpose(1, 0, 2).reshape(w.shape[0] // k, -1)

    gu = np.concatenate([a["L0_ffn_w_gate"], a["L0_ffn_w_up"]], axis=2)
    sgu = np.concatenate([a["L0_ffn_ws_gate"], a["L0_ffn_ws_up"]], axis=1)
    sdn = a["L0_ffn_ws_down"]
    return {
        "x": a["L0_attn_x"].reshape(T, D),
        "consts": constants(),
        "wr": rows(a["L0_ffn_w_router"], KD),
        "wqkv": rows(a["L0_attn_W_qkv"].T, KD),
        "wout": rows(a["L0_attn_W_out"].T, KD),
        "wsgu": rows(sgu, KD),
        "wsdn_a": rows(sdn[0:2 * P], 2),
        "wsdn_b": sdn[2 * P:],
        "egu": gu.reshape(E, KD, P, 2 * F).transpose(2, 0, 1, 3).reshape(P, E, EG),
        "edn": a["L0_ffn_w_down"].reshape(E, 2, FH, D).transpose(2, 0, 1, 3).reshape(FH, E, ED),
    }


def kernel(**inputs):
    import numpy as np
    import concourse.bacc as bacc
    from concourse.bass_utils import run_bass_kernel_spmd

    nc = bacc.Bacc("TRN2", target_bir_lowering=False, num_devices=1)
    arrays = {n: np.ascontiguousarray(v) for n, v in laid_out({k: np.asarray(v) for k, v in inputs.items()}).items()}
    args = [nc.dram_tensor(n, v.shape, F32, kind="ExternalInput").ap() for n, v in arrays.items()]
    out = nc.dram_tensor("out", (T, D), F32, kind="ExternalOutput").ap()
    build(nc, *args, out)
    r = run_bass_kernel_spmd(nc, [arrays], core_ids=[0])
    return r.results[0]["out"].reshape(4, T // 4, D)
```

```python
from contextlib import ExitStack

import concourse.bass as bass
from concourse import mybir

F32 = mybir.dt.float32
F32R = mybir.dt.float32r
F16 = mybir.dt.float16
I32 = mybir.dt.int32
ALU = mybir.AluOpType
ACT = mybir.ActivationFunctionType
AX = mybir.AxisListType.X

EARLY = 2
P = 128
T = 2048
D = 256
KD = D // P
NT = T // P
GT = 512
NG = T // GT
TG = GT // P
E = 8
F = 176
FH = F // 2
FS = 352
SCH = [(0, 128), (128, 128), (256, 96)]
NS = 39
SCALE = 2.5
HD_SCALE = 0.25
EPS_LN = 1e-5
EPS_ATT = 1e-9

C_ID, C_TRI, C_DESC, C_RESET, C_THR, C_I40, C_I128, C_TOK, C_END = (
    0, 128, 256, 264, 392, 408, 448, 576, 608)

W_OUT = KD * 3 * D
W_SDN = KD * 2 * FS
W_COLS = W_SDN + 3 * D
EG = KD * 2 * F
ED = 2 * D

B_K, B_V, B_Q, B_PROJ, B_ROUTE = 0, 1, 2, 6, 7
L_OFF, R_OFF, T_OFF, TAB_OFF = 0, 128, 256, 384

(W_EQ, W_EK, W_RQ, W_RK, W_NUM, W_P, W_KC, W_KVC, W_SLOTS) = (0, 1, 2, 4, 6, 8, 10, 12, 14)


UNITS = 2 * NG
CHUNKS = 3 * NG
WD = (0, W_OUT, W_OUT + KD * D)
WS = (0, W_SDN, W_SDN + 2 * D, W_COLS)
WS_ROWS = (P, P, SCH[2][1])


def wait_if(eng, s, n):
    if not (isinstance(n, int) and n <= 0):
        eng.wait_ge(s, n)


def proj_bank(n):
    return B_ROUTE if n in (5, 7) else B_PROJ


def build(nc, x, consts, wr, wqkv, wout, wsgu, wsdn_a, wsdn_b, egu, edn, out):
    xn_dram = nc.dram_tensor("xn_rows", (T, D), F32).ap()
    y_dram = nc.dram_tensor("y_rows", (NS * P, D), F32).ap()

    with ExitStack() as ctx:
        def sb(name, shape, dt):
            return ctx.enter_context(nc.sbuf_tensor(name, shape, dt))

        def sem(name):
            return ctx.enter_context(nc.semaphore(name))

        ps = ctx.enter_context(nc.psum_tensor("ps", [P, 8, 512], F32))
        x_acc = sb("x_acc", [P, NT, D], F32)
        xT_hi = sb("xT_hi", [P, KD, T], F32R)
        xT_lo = sb("xT_lo", [P, KD, T], F32R)
        w_hi = sb("w_hi", [P, W_COLS], F32R)
        w_lo = sb("w_lo", [P, W_COLS], F32R)
        wr_raw = sb("wr_raw", [P, KD * E], F32)
        wr_hi = sb("wr_hi", [P, KD * E], F32R)
        wr_lo = sb("wr_lo", [P, KD * E], F32R)
        eg_hi = sb("eg_hi", [P, E * EG], F32R)
        eg_lo = sb("eg_lo", [P, E * EG], F32R)
        ed_hi = sb("ed_hi", [FH, E * ED], F32R)
        ed_lo = sb("ed_lo", [FH, E * ED], F32R)
        e_raw = sb("e_raw", [P, EG + ED], F32)
        t_hi = sb("t_hi", [P, 4, GT], F32R)
        t_lo = sb("t_lo", [P, 4, GT], F32R)
        work = sb("work", [P, W_SLOTS, GT], F32)
        xg = sb("xg", [P, 4, D], F32)
        cst = sb("cst", [P, C_END], F32)
        ones = sb("ones", [P, P], F32)
        stats = sb("stats", [P, TG, 6], F32)
        mv = sb("mv", [P, NT, 2], F32)
        std = sb("std", [P, NT], F32)
        rz = sb("rz", [P, NT, E], F32)
        rp = sb("rp", [P, NT, E], F32)
        rc = sb("rc", [P, NT, E], F32)
        m1 = sb("m1", [P, NT, E], F32)
        m2 = sb("m2", [P, NT, E], F32)
        small = sb("small", [P, 8, NT], F32)
        wgt = sb("wgt", [P, 2, NT], F32)
        tot = sb("tot", [P, E, NT], F32)
        etab_w = sb("etab_w", [1, NS, E], F32)
        pm_i = sb("pm_i", [P, 2 * NT], I32)
        eps_col = sb("eps_col", [P, 1], F32)
        slot = sb("slot", [P, 2 * NT], F32)
        slot_i = sb("slot_i", [P, 2 * NT], I32)
        pm = sb("pm", [P, 2 * NT], F32)
        jm = sb("jm", [P, 2 * NT], F32)
        hotj = sb("hotj", [P, 2 * NT, NS], F16)
        tok_i = sb("tok_i", [P, NS], I32)
        etab_f = sb("etab_f", [1, NS], F32)
        etab = sb("etab", [1, NS + 2], I32)

        x_in = [sem(f"x_in{g}") for g in range(NG)]
        cst_in, wr_in, wd_in, ws_in, e_in = (sem(n) for n in ("cst_in", "wr_in", "wd_in", "ws_in", "e_in"))
        xn_out, acc_out = sem("xn_out"), sem("acc_out")
        stat_s, var_ready, std_ready, rstd_ready, xn_ready = (
            sem(n) for n in ("stat_s", "var_ready", "std_ready", "rstd_ready", "xn_ready"))
        tr_ready, xT_hi_ready, xT_lo_ready, logits_ready = (
            sem(n) for n in ("tr_ready", "xT_hi_ready", "xT_lo_ready", "logits_ready"))
        ones_ready, wr_hi_s, wr_lo_s = sem("ones_ready"), sem("wr_hi_s"), sem("wr_lo_s")
        wd_hi_s, wd_lo_s, ws_hi_s, ws_lo_s, e_hi_s, e_lo_s = (
            sem(n) for n in ("wd_hi_s", "wd_lo_s", "ws_hi_s", "ws_lo_s", "e_hi_s", "e_lo_s"))
        k_ready, v_ready, q_ready, k_act, q_act = (
            sem(n) for n in ("k_ready", "v_ready", "q_ready", "k_act", "q_act"))
        phik_s, kv_s, kc_s, kvc_s, phiq_s = (sem(n) for n in ("phik_s", "kv_s", "kc_s", "kvc_s", "phiq_s"))
        den_s, num_s, ln_s, rec_s, out_s, o_hi, o_lo = (
            sem(n) for n in ("den_s", "num_s", "ln_s", "rec_s", "out_s", "o_hi", "o_lo"))
        proj_ready, acc_done = sem("proj_ready"), sem("acc_done")
        rt, z_ready, ez_ready, mask_ready, prefix_ready = (
            sem(n) for n in ("rt", "z_ready", "ez_ready", "mask_ready", "prefix_ready"))
        hot_ready, hot_used, tab_ready, tok_ready, etab_ready, slots_ready = (
            sem(n) for n in ("hot_ready", "hot_used", "tab_ready", "tok_ready", "etab_ready", "slots_ready"))
        gathered = [sem(f"gathered{b}") for b in range(4)]
        xt_ready, xt_hi_s, xt_lo_s, gu_ready, silu_s, h_s = (
            sem(n) for n in ("xt_ready", "xt_hi_s", "xt_lo_s", "gu_ready", "silu_s", "h_s"))
        ht_ready, ht_hi_s, ht_lo_s, y_ready, y_copied = (
            sem(n) for n in ("ht_ready", "ht_hi_s", "ht_lo_s", "y_ready", "y_copied"))
        y_stored = [sem(f"y_stored{b}") for b in range(2)]
        g_ready, u_ready, s_silu, s_h, s_hi, s_lo, down_ready = (
            sem(n) for n in ("g_ready", "u_ready", "s_silu", "s_h", "s_hi", "s_lo", "down_ready"))
        y_in = [sem(f"y_in{b}") for b in range(4)]
        add1, add2, fin_s = sem("add1"), sem("add2"), sem("fin_s")

        lg_ready, lg_copied = sem("lg_ready"), sem("lg_copied")

        def flat(i, n=1):
            return work[:, i:i + n, :].rearrange("p a b -> p (a b)")

        wd_raw = flat(W_NUM, 4)
        ws_raw = flat(0, 5)[:, 0:W_COLS]
        xn_rows = flat(W_KC, 4).rearrange("p (i d) -> p i d", d=D)

        lg = work[0:E, 3:6:2, :]

        s_buf = work[:, W_KC, 0:2 * F].rearrange("p (b f) -> p b f", b=2)
        h_buf = work[:, W_KC + 1, 0:2 * F].rearrange("p (b f) -> p b f", b=2)
        y_buf = work[:, W_P, :].rearrange("p (b f) -> p b f", b=2)

        def xt(t, b):
            return t[:, 0, b * D:(b + 1) * D]

        def ht(t, b):
            return t[0:FH, 1, b * D:(b + 1) * D]

        yg = flat(W_KVC, 2).rearrange("p (b d) -> p b d", b=4)

        block = ctx.enter_context(nc.Block())

        @block.sync
        def _(sp):
            xv = x.rearrange("(t p) d -> p t d", p=P)
            ov = out.rearrange("(t p) d -> p t d", p=P)
            nv = xn_dram.rearrange("(t p) d -> p t d", p=P)
            yv = y_dram.rearrange("(t p) d -> p t d", p=P)

            sp.dma_start(x_acc[:, 0:TG, :], xv[:, 0:TG, :]).then_inc(x_in[0], 16)
            sp.dma_start(cst[:], consts).then_inc(cst_in, 16)
            sp.dma_start(wr_raw[:], wr).then_inc(wr_in, 16)
            for g in range(1, NG):
                sp.dma_start(x_acc[:, g * TG:(g + 1) * TG, :],
                             xv[:, g * TG:(g + 1) * TG, :]).then_inc(x_in[g], 16)
            sp.dma_start(wd_raw[:, 0:W_OUT], wqkv).then_inc(wd_in, 16)
            sp.dma_start(wd_raw[:, W_OUT:W_OUT + KD * D], wout).then_inc(wd_in, 16)

            def expert(e):
                if e:
                    sp.wait_ge(e_hi_s, 2 * e)
                    sp.wait_ge(e_lo_s, 2 * e)
                sp.dma_start(e_raw[:, 0:EG], egu[:, e, :]).then_inc(e_in, 16)
                sp.dma_start(e_raw[0:FH, EG:EG + ED], edn[:, e, :]).then_inc(e_in, 16)

            expert(0)
            for g in range(NG):
                sp.wait_ge(xn_ready, TG * (g + 1))
                sp.dma_start(nv[:, g * TG:(g + 1) * TG, :],
                             xn_rows[:, TG * (g % 2):TG * (g % 2 + 1), :]).then_inc(xn_out, 16)
                if g < NG - 1:
                    sp.wait_ge(xn_out, 16 * (g + 1))
            for e in range(1, E):
                expert(e)
            sp.wait_ge(o_lo, 2 * NG)
            sp.dma_start(ws_raw[:, 0:W_SDN], wsgu).then_inc(ws_in, 16)
            sp.dma_start(ws_raw[:, W_SDN:W_SDN + 2 * D], wsdn_a).then_inc(ws_in, 16)
            sp.dma_start(ws_raw[0:SCH[2][1], W_SDN + 2 * D:W_COLS], wsdn_b).then_inc(ws_in, 16)
            with sp.Fori(0, NS // 2) as j:
                for b in range(2):
                    sp.wait_ge(y_copied, j * 2 + (b + 1))
                    sp.dma_start(yv[:, bass.ds(j * 2 + b, 1), :],
                                 y_buf[:, b:b + 1, :]).then_inc(y_stored[b], 16)
            sp.wait_ge(y_copied, NS)
            sp.dma_start(yv[:, NS - 1:NS, :], y_buf[:, 0:1, :]).then_inc(y_stored[0], 16)
            for g in range(NG):
                for h in range(2):
                    sp.wait_ge(fin_s, 2 * g + h + 1)
                    a = TG * g + 2 * h
                    sp.dma_start(ov[:, a:a + 2, :], x_acc[:, a:a + 2, :]).then_inc(acc_out, 16)
            sp.wait_ge(acc_out, 16 * 2 * NG)
            sp.wait_ge(xn_out, 16 * NG)

        @block.gpsimd
        def _(pool):
            q = nc.gpsimd
            q.memset(ones[:], 1.0).then_inc(ones_ready, 1)
            q.memset(eps_col[:], EPS_ATT).then_inc(ones_ready, 1)

            def low(dst, raw, high, done):
                q.tensor_tensor(dst, raw, high.bitcast(F32), ALU.subtract).then_inc(done, 1)

            q.memset(etab[:], 0).then_inc(ones_ready, 1)
            pool.wait_ge(wr_hi_s, 1)
            low(wr_lo[:], wr_raw[:], wr_hi[:], wr_lo_s)
            for h in range(2):
                pool.wait_ge(wd_hi_s, h + 1)
                low(w_lo[:, WD[h]:WD[h + 1]], wd_raw[:, WD[h]:WD[h + 1]], w_hi[:, WD[h]:WD[h + 1]], wd_lo_s)

            def expert_low(u):
                pool.wait_ge(e_hi_s, 2 * u + 2)
                low(eg_lo[:, u * EG:(u + 1) * EG], e_raw[:, 0:EG], eg_hi[:, u * EG:(u + 1) * EG], e_lo_s)
                low(ed_lo[:, u * ED:(u + 1) * ED], e_raw[0:FH, EG:EG + ED], ed_hi[:, u * ED:(u + 1) * ED], e_lo_s)

            def gather(t):
                q.indirect_dma_start(
                    out=xg[:, t % 4, :], out_offset=None, in_=xn_dram,
                    in_offset=bass.IndirectOffsetOnAxis(ap=tok_i[:, t:t + 1], axis=0),
                ).then_inc(gathered[t % 4], 16)

            for e in range(EARLY):
                expert_low(e)
            for u in range(UNITS):
                c = u % 2
                pool.wait_ge(phiq_s, u + 1)
                pool.wait_ge(kc_s, u + 1)
                if u >= 2:
                    pool.wait_ge(out_s, u - 1)
                q.tensor_tensor(work[:, W_P + c, :], work[:, W_RQ + c, :], work[:, W_KC + c, :],
                                ALU.mult).then_inc(den_s, 1)
                pool.wait_ge(kvc_s, u + 1)
                if u >= 2:
                    pool.wait_ge(o_lo, u - 1)
                q.tensor_tensor(work[:, W_NUM + c, :], work[:, W_RQ + c, :], work[:, W_KVC + c, :],
                                ALU.mult).then_inc(num_s, 1)
                if u + EARLY < E:
                    expert_low(u + EARLY)
                if u == UNITS - 2:
                    pool.wait_ge(tok_ready, 1)
                    pool.wait_ge(xn_out, 16 * NG)
                    for t in range(4):
                        gather(t)

            def shared_low(h):
                n = WS_ROWS[h]
                pool.wait_ge(ws_hi_s, h + 1)
                low(w_lo[0:n, WS[h]:WS[h + 1]], ws_raw[0:n, WS[h]:WS[h + 1]], w_hi[0:n, WS[h]:WS[h + 1]], ws_lo_s)

            for t in range(4, NS):
                pool.wait_ge(xt_ready, t - 3)
                gather(t)
                if 8 <= t < 11:
                    shared_low(t - 8)

            for b in range(2):
                pool.wait_ge(y_stored[b], 16 * ((NS + 1 - b) // 2))
            for i in range(NT):
                for k in range(2):
                    b = (2 * i + k) % 4
                    if i >= 2:
                        pool.wait_ge((add1, add2)[k], i - 1)
                    q.indirect_dma_start(
                        out=yg[:, b, :], out_offset=None, in_=y_dram,
                        in_offset=bass.IndirectOffsetOnAxis(ap=slot_i[:, k * NT + i:k * NT + i + 1], axis=0),
                    ).then_inc(y_in[b], 16)

        @block.scalar
        def _(act):
            a = nc.scalar

            def high(dst, raw, done):
                a.activation(dst, raw, ACT.Copy).then_inc(done, 1)

            def sqrt(g):
                act.wait_ge(var_ready, g + 1)
                a.activation(std[:, g * TG:(g + 1) * TG], mv[:, g * TG:(g + 1) * TG, 1],
                             ACT.Sqrt).then_inc(std_ready, 1)

            def xT_high(g):
                for k in range(KD):
                    act.wait_ge(tr_ready, 2 * g + k + 1)
                    high(xT_hi[:, k, g * GT:(g + 1) * GT], ps[:, 2 + 2 * (g % 2) + k, :], xT_hi_ready)

            def logits_copy(g):
                act.wait_ge(lg_ready, g + 1)
                if g >= 2:
                    act.wait_ge(logits_ready, g - 1)
                a.activation(lg[:, g % 2, :], ps[0:E, B_PROJ, :], ACT.Copy).then_inc(lg_copied, 1)

            act.wait_ge(wr_in, 16)
            high(wr_hi[:], wr_raw[:], wr_hi_s)
            sqrt(0)
            sqrt(1)
            xT_high(0)
            sqrt(2)
            xT_high(1)
            logits_copy(0)
            sqrt(3)
            act.wait_ge(wd_in, 32)
            for h in range(2):
                high(w_hi[:, WD[h]:WD[h + 1]], wd_raw[:, WD[h]:WD[h + 1]], wd_hi_s)
            xT_high(2)
            logits_copy(1)
            xT_high(3)
            logits_copy(2)

            def expert_high(e):
                act.wait_ge(e_in, 32 * (e + 1))
                high(eg_hi[:, e * EG:(e + 1) * EG], e_raw[:, 0:EG], e_hi_s)
                high(ed_hi[:, e * ED:(e + 1) * ED], e_raw[0:FH, EG:EG + ED], e_hi_s)

            for e in range(EARLY):
                expert_high(e)
            logits_copy(3)

            def k_parts(u):
                c, b = u % 2, 3 * (u % 2)
                act.wait_ge(k_ready, u + 1)
                if u >= 1:
                    act.wait_ge(kvc_s, u)
                a.activation(work[:, W_EK, :], ps[:, b + B_K, :], ACT.Exp)
                a.activation(work[:, W_RK + c, :], ps[:, b + B_K, :], ACT.Relu).then_inc(k_act, 1)

            def q_parts(u):
                c, b = u % 2, 3 * (u % 2)
                act.wait_ge(q_ready, u + 1)
                if u >= 1:
                    act.wait_ge(phiq_s, u)
                if u >= 2:
                    act.wait_ge(num_s, u - 1)
                a.activation(work[:, W_EQ, :], ps[:, b + B_Q, :], ACT.Exp)
                a.activation(work[:, W_RQ + c, :], ps[:, b + B_Q, :], ACT.Relu).then_inc(q_act, 1)

            def reciprocal(u):
                d = work[:, W_P + u % 2, :]
                act.wait_ge(den_s, u + 1)
                a.activation(d, d, ACT.Ln, bias=eps_col[:, 0:1]).then_inc(ln_s, 1)
                act.wait_ge(ln_s, u + 1)
                a.activation(d, d, ACT.Exp, scale=-1.0).then_inc(rec_s, 1)

            def out_high(u):
                act.wait_ge(out_s, u + 1)
                if u >= 4:
                    act.wait_ge(proj_ready, 2 * ((u - 4) // 2 + 1))
                high(t_hi[:, u % 4, :], work[:, W_NUM + u % 2, :], o_hi)

            a.preload_act_table_set("natural_log_exp_and_others")
            act.wait_ge(ones_ready, 3)
            for u in range(UNITS + 1):
                if u < UNITS:
                    k_parts(u)
                if u >= 2:
                    out_high(u - 2)
                if u < UNITS:
                    q_parts(u)
                if u == 0:
                    act.wait_ge(z_ready, 1)
                    a.activation(rz[:], rz[:], ACT.Exp).then_inc(ez_ready, 1)
                if 1 <= u:
                    reciprocal(u - 1)
                if u + EARLY < E:
                    expert_high(u + EARLY)

            def shared_high():
                act.wait_ge(proj_ready, 2 * NG)
                act.wait_ge(ws_in, 48)
                for h in range(3):
                    n = WS_ROWS[h]
                    high(w_hi[0:n, WS[h]:WS[h + 1]], ws_raw[0:n, WS[h]:WS[h + 1]], ws_hi_s)

            def h_high(t, b):
                act.wait_ge(ht_ready, t + 1)
                wait_if(act, y_ready, t - 1)
                high(ht(t_hi, b), ps[0:FH, 4 + b, 0:D], ht_hi_s)

            def x_high(t, b):
                act.wait_ge(xt_ready, t + 1)
                wait_if(act, gu_ready, t - 1)
                high(xt(t_hi, b), ps[:, b, 0:D], xt_hi_s)

            def silu(t, b):
                act.wait_ge(gu_ready, t + 1)
                wait_if(act, h_s, t - 1)
                a.activation(s_buf[:, b, :], ps[:, 2 + b, 0:F], ACT.Silu).then_inc(silu_s, 1)

            def y_copy(t, b, stored):
                act.wait_ge(y_ready, t + 1)
                wait_if(act, y_stored[b], stored)
                a.activation(y_buf[:, b, :], ps[:, 6 + b, 0:D], ACT.Copy).then_inc(y_copied, 1)

            def r_step(j, b, first=False, behind=True, ahead=True):
                t = j * 2 + b
                if ahead:
                    x_high(t + 1, 1 - b)
                silu(t, b)
                if not first:
                    h_high(t - 1, 1 - b)
                if behind:
                    y_copy(t - 2, b, (j - 1) * 16)

            a.preload_act_table(ACT.Silu)
            act.wait_ge(proj_ready, 6)
            x_high(0, 0)
            out_high(UNITS - 1)
            r_step(0, 0, first=True, behind=False)
            r_step(0, 1, behind=False)
            shared_high()
            with act.Fori(1, NS // 2) as j:
                for b in range(2):
                    r_step(j, b)
            r_step(NS // 2, 0, ahead=False)
            h_high(NS - 1, 0)
            y_copy(NS - 2, 1, 16 * (NS // 2 - 1))
            y_copy(NS - 1, 0, 16 * (NS // 2))

            def s_high(i):
                n = SCH[i % 3][1]
                act.wait_ge(s_h, i + 1)
                if i < 4:
                    act.wait_ge(y_ready, NS)
                else:
                    act.wait_ge(down_ready, 2 * ((i - 4) // 3 + 1))
                high(t_hi[0:n, i % 4, :], work[0:n, 2 + i % 2, :], s_hi)

            act.wait_ge(ws_lo_s, 3)
            for i in range(CHUNKS):
                n = SCH[i % 3][1]
                act.wait_ge(g_ready, i + 1)
                if i >= 2:
                    act.wait_ge(s_h, i - 1)
                a.activation(work[0:n, i % 2, :], ps[0:n, 2 * (i % 2), :], ACT.Silu).then_inc(s_silu, 1)
                if i >= 1:
                    s_high(i - 1)
            s_high(CHUNKS - 1)

        @block.vector
        def _(dve):
            v = nc.vector

            def low(dst, full, high, done):
                v.tensor_tensor(dst, full, high.bitcast(F32), ALU.subtract).then_inc(done, 1)

            def row_stats(g):
                dve.wait_ge(x_in[g], 16)
                if g:
                    dve.wait_ge(stat_s, 8 * g)
                for i in range(TG):
                    v.bn_stats(stats[:, i, :], x_acc[:, g * TG + i, :]).then_inc(stat_s, 1)
                dve.wait_ge(stat_s, 8 * g + 4)
                for i in range(TG):
                    v.bn_aggr(mv[:, g * TG + i, :], stats[:, i, :]).then_inc(stat_s, 1)
                dve.wait_ge(stat_s, 8 * g + 8)
                var = mv[:, g * TG:(g + 1) * TG, 1]
                v.tensor_scalar(var, var, EPS_LN, None, ALU.add).then_inc(var_ready, 1)

            def normed(g):
                dve.wait_ge(std_ready, g + 1)
                r = std[:, g * TG:(g + 1) * TG]
                v.reciprocal(r, r).then_inc(rstd_ready, 1)
                dve.wait_ge(rstd_ready, g + 1)
                if g >= 2:
                    dve.wait_ge(xn_out, 16 * (g - 1))
                    dve.wait_ge(tr_ready, 2 * (g - 1))
                for i in range(g * TG, (g + 1) * TG):
                    v.tensor_scalar(xn_rows[:, i % 8, :], x_acc[:, i, :], mv[:, i, 0:1], std[:, i:i + 1],
                                    ALU.subtract, ALU.mult).then_inc(xn_ready, 1)

            def xT_low(g):
                for k in range(KD):
                    dve.wait_ge(xT_hi_ready, 2 * g + k + 1)
                    cols = slice(g * GT, (g + 1) * GT)
                    low(xT_lo[:, k, cols], ps[:, 2 + 2 * (g % 2) + k, :], xT_hi[:, k, cols], xT_lo_ready)

            row_stats(0)
            row_stats(1)
            normed(0)
            row_stats(2)
            normed(1)
            xT_low(0)
            row_stats(3)
            normed(2)
            xT_low(1)
            normed(3)
            xT_low(2)
            xT_low(3)

            n_rt = [0]

            def link(ins):
                n_rt[0] += 1
                ins.then_inc(rt, 1)
                dve.wait_ge(rt, n_rt[0])

            def over_e(ap):
                return ap.unsqueeze(2).broadcast_to([P, NT, E])

            logits = ps[:, B_ROUTE, L_OFF:L_OFF + NT * E].rearrange("p (t e) -> p t e", e=E)
            desc = cst[:, C_DESC:C_DESC + E].unsqueeze(1).broadcast_to([P, NT, E])
            mx, sm, p1, p2, c1, ws = (small[:, n, :] for n in range(6))

            def route_logits():
                dve.wait_ge(logits_ready, NG)
                link(v.tensor_reduce(mx, logits, AX, ALU.max))
                v.tensor_tensor(rz[:], logits, over_e(mx), ALU.subtract).then_inc(z_ready, 1)

            def first_max(mask, top):
                link(v.tensor_reduce(top, rp[:], AX, ALU.max))
                link(v.tensor_tensor(rc[:], rp[:], over_e(top), ALU.is_equal))
                link(v.tensor_tensor(rc[:], rc[:], desc, ALU.mult))
                link(v.tensor_reduce(c1, rc[:], AX, ALU.max))
                link(v.tensor_tensor(mask, rc[:], over_e(c1), ALU.is_equal))

            def route_top2():
                dve.wait_ge(ez_ready, 1)
                link(v.tensor_reduce(sm, rz[:], AX, ALU.add))
                link(v.reciprocal(sm, sm))
                link(v.tensor_tensor(rp[:], rz[:], over_e(sm), ALU.mult))
                dve.wait_ge(cst_in, 16)
                first_max(m1[:], p1)
                link(v.scalar_tensor_tensor(out=rp[:], in0=m1[:], scalar=-2.0, in1=rp[:],
                                            op0=ALU.mult, op1=ALU.add))
                first_max(m2[:], p2)
                v.tensor_tensor(rz[:], m1[:], m2[:], ALU.add).then_inc(mask_ready, 1)
                link(v.tensor_tensor(ws, p1, p2, ALU.add))
                link(v.reciprocal(ws, ws))
                for k, pk in enumerate((p1, p2)):
                    link(v.scalar_tensor_tensor(out=wgt[:, k, :], in0=pk, scalar=SCALE, in1=ws,
                                                op0=ALU.mult, op1=ALU.mult))

            def route_slots():
                et = rc[:].rearrange("p t e -> p (t e)").rearrange("p (e t) -> p e t", e=E)
                cum = rp[:].rearrange("p t e -> p (t e)").rearrange("p (e t) -> p e t", e=E)
                one = ones[:, 0:E]
                dve.wait_ge(prefix_ready, 1)
                link(v.tensor_copy(et, ps[:, B_ROUTE, T_OFF:T_OFF + NT * E].rearrange("p (t e) -> p e t", e=E)))
                link(v.tensor_tensor_scan(rp[:].rearrange("p t e -> p (t e)"), cst[:, C_RESET:C_RESET + NT * E],
                                          rc[:].rearrange("p t e -> p (t e)"), 0.0, ALU.mult, ALU.add))
                thr = cst[:, C_THR:C_THR + NT].unsqueeze(1).broadcast_to([P, E, NT])
                link(v.tensor_tensor(tot[:, :, 0:NT], cum[:, :, NT - 1:NT].broadcast_to([P, E, NT]), thr, ALU.is_gt))
                link(v.tensor_reduce(small[:, 6, 0:E], tot[:, :, 0:NT], AX, ALU.add))
                dve.wait_ge(ones_ready, 3)
                link(v.tensor_tensor_scan(small[:, 6, E:2 * E], one, small[:, 6, 0:E], 0.0, ALU.mult, ALU.add))
                link(v.tensor_tensor(small[:, 7, 0:E], small[:, 6, E:2 * E], small[:, 6, 0:E], ALU.subtract))
                link(v.tensor_scalar(small[:, 7, 0:E], small[:, 7, 0:E], float(P), None, ALU.mult))
                link(v.tensor_tensor(rp[:].rearrange("p t e -> p (t e)"), rp[:].rearrange("p t e -> p (t e)"),
                                     rc[:].rearrange("p t e -> p (t e)"), ALU.subtract))
                link(v.tensor_tensor(cum, cum, small[:, 7, 0:E].unsqueeze(2).broadcast_to([P, E, NT]), ALU.add))
                before = ps[:, B_ROUTE, R_OFF:R_OFF + NT * E].rearrange("p (t e) -> p t e", e=E)
                link(v.tensor_tensor(rc[:], before, cum.rearrange("p e t -> p t e"), ALU.add))
                for k, m in enumerate((m1, m2)):
                    link(v.tensor_tensor(m[:], m[:], rc[:], ALU.mult))
                    link(v.tensor_reduce(slot[:, k * NT:(k + 1) * NT], m[:], AX, ALU.add))
                v.tensor_copy(slot_i[:], slot[:]).then_inc(slots_ready, 1)
                dve.wait_ge(slots_ready, 1)
                link(v.tensor_scalar(pm_i[:], slot_i[:], P - 1, None, ALU.bitwise_and))
                link(v.tensor_copy(pm[:], pm_i[:]))
                link(v.tensor_tensor(jm[:], slot[:], pm[:], ALU.subtract))
                link(v.tensor_scalar(jm[:], jm[:], 1.0 / P, None, ALU.mult))
                j40 = cst[0:1, C_I40:C_I40 + NS].unsqueeze(2).broadcast_to([1, NS, E])
                ends = small[0:1, 6, E:2 * E].unsqueeze(1).broadcast_to([1, NS, E])
                link(v.tensor_tensor(etab_w[:], j40, ends, ALU.is_ge))
                link(v.tensor_reduce(etab_f[:], etab_w[:], AX, ALU.add))
                v.tensor_scalar(etab[:, 2:NS + 2], etab_f[:], float(E - 1), None, ALU.min).then_inc(etab_ready, 1)

            hotp = xg[:].rearrange("p b d -> p (b d)").bitcast(F16).rearrange("p (i s) -> p i s", s=P)

            def route_hot(k):
                if k == 0:
                    i40 = cst[:, C_I40:C_I40 + NS].unsqueeze(1).broadcast_to([P, 2 * NT, NS])
                    link(v.tensor_tensor(hotj[:], jm[:].unsqueeze(2).broadcast_to([P, 2 * NT, NS]), i40, ALU.is_equal))
                    tok = cst[:, C_TOK:C_TOK + 2 * NT].unsqueeze(2).broadcast_to([P, 2 * NT, NS])
                    link(v.tensor_tensor(hotj[:], hotj[:], tok, ALU.mult))
                else:
                    dve.wait_ge(hot_used, 1)
                i128 = cst[:, C_I128:C_I128 + P].unsqueeze(1).broadcast_to([P, NT, P])
                v.tensor_tensor(hotp, pm[:, k * NT:(k + 1) * NT].unsqueeze(2).broadcast_to([P, NT, P]), i128,
                                ALU.is_equal).then_inc(hot_ready, 1)

            def route_table():
                dve.wait_ge(hot_used, 2)
                v.tensor_copy(tok_i[:], ps[:, B_ROUTE, TAB_OFF:TAB_OFF + NS]).then_inc(tok_ready, 1)

            def keys(u):
                c, b = u % 2, 3 * (u % 2)
                ek, rk = work[:, W_EK, :], work[:, W_RK + c, :]
                kc, kvc = work[:, W_KC + c, :], work[:, W_KVC + c, :]
                dve.wait_ge(k_act, u + 1)
                v.scalar_tensor_tensor(out=rk, in0=ek, scalar=1.0, in1=rk, op0=ALU.min,
                                       op1=ALU.add).then_inc(phik_s, 1)
                dve.wait_ge(phik_s, u + 1)
                dve.wait_ge(v_ready, u + 1)
                v.tensor_tensor(ek, rk, ps[:, b + B_V, :], ALU.mult).then_inc(kv_s, 1)
                if u >= 2:
                    dve.wait_ge(den_s, u - 1)
                else:
                    dve.wait_ge(xn_out, 16 * NG)
                one = ones[:, 0:1].broadcast_to([P, GT])
                v.tensor_tensor_scan(kc, one, rk, 0.0, ALU.mult,
                                     ALU.add).then_inc(kc_s, 1)
                dve.wait_ge(kv_s, u + 1)
                if u >= 2:
                    dve.wait_ge(num_s, u - 1)
                v.tensor_tensor_scan(kvc, one, ek, 0.0, ALU.mult,
                                     ALU.add).then_inc(kvc_s, 1)

            def queries(u):
                c = u % 2
                rq = work[:, W_RQ + c, :]
                dve.wait_ge(q_act, u + 1)
                v.scalar_tensor_tensor(out=rq, in0=work[:, W_EQ, :], scalar=1.0, in1=rq, op0=ALU.min,
                                       op1=ALU.add).then_inc(phiq_s, 1)

            def divided(u):
                n = work[:, W_NUM + u % 2, :]
                dve.wait_ge(rec_s, u + 1)
                dve.wait_ge(num_s, u + 1)
                v.tensor_tensor(n, n, work[:, W_P + u % 2, :], ALU.mult).then_inc(out_s, 1)

            def out_low(u):
                dve.wait_ge(o_hi, u + 1)
                low(t_lo[:, u % 4, :], work[:, W_NUM + u % 2, :], t_hi[:, u % 4, :], o_lo)

            def add_proj(n):
                dve.wait_ge(proj_ready, n + 1)
                two = x_acc[:, 2 * n:2 * n + 2, :].rearrange("p a b -> p (a b)")
                v.scalar_tensor_tensor(out=two, in0=ps[:, proj_bank(n), :], scalar=HD_SCALE, in1=two, op0=ALU.mult,
                                       op1=ALU.add).then_inc(acc_done, 1)

            route_logits()
            dve.wait_ge(ones_ready, 3)
            for u in range(UNITS + 2):
                if u < UNITS:
                    keys(u)
                if u >= 4:
                    add_proj(u - 4)
                if u < UNITS:
                    queries(u)
                if u >= 2:
                    out_low(u - 2)
                if 1 <= u <= UNITS:
                    divided(u - 1)
                if u == 0:
                    route_top2()
                if u == 2:
                    route_slots()
                if u == 3:
                    route_hot(0)
                if u == 4:
                    route_hot(1)
                if u == 5:
                    route_table()
            def h_low(t, b):
                dve.wait_ge(ht_hi_s, t + 1)
                low(ht(t_lo, b), ps[0:FH, 4 + b, 0:D], ht(t_hi, b), ht_lo_s)

            def x_low(t, b):
                dve.wait_ge(xt_hi_s, t + 1)
                low(xt(t_lo, b), ps[:, b, 0:D], xt(t_hi, b), xt_lo_s)

            def hidden(t, b):
                dve.wait_ge(silu_s, t + 1)
                wait_if(dve, ht_ready, t - 1)
                v.tensor_tensor(h_buf[:, b, :], s_buf[:, b, :], ps[:, 2 + b, F:2 * F], ALU.mult).then_inc(h_s, 1)

            def r_step(j, b, first=False, behind=True, ahead=True):
                t = j * 2 + b
                if ahead:
                    x_low(t + 1, 1 - b)
                hidden(t, b)
                if not first:
                    h_low(t - 1, 1 - b)

            x_low(0, 0)
            r_step(0, 0, first=True, behind=False)
            r_step(0, 1, behind=False)
            for n in range(6, 8):
                add_proj(n)
            with dve.Fori(1, NS // 2) as j:
                for b in range(2):
                    r_step(j, b)
            r_step(NS // 2, 0, ahead=False)
            h_low(NS - 1, 0)

            def s_hidden(i):
                n = SCH[i % 3][1]
                dve.wait_ge(s_silu, i + 1)
                dve.wait_ge(u_ready, i + 1)
                if i >= 2:
                    dve.wait_ge(s_lo, i - 1)
                v.tensor_tensor(work[0:n, 2 + i % 2, :], work[0:n, i % 2, :], ps[0:n, 2 * (i % 2) + 1, :],
                                ALU.mult).then_inc(s_h, 1)

            def s_low(i):
                n = SCH[i % 3][1]
                dve.wait_ge(s_hi, i + 1)
                low(t_lo[0:n, i % 4, :], work[0:n, 2 + i % 2, :], t_hi[0:n, i % 4, :], s_lo)

            def add_routed(i):
                for k in range(2):
                    b = (2 * i + k) % 4
                    dve.wait_ge(y_in[b], 16 * (i // 2 + 1))
                    if k:
                        dve.wait_ge(add1, i + 1)
                    v.scalar_tensor_tensor(out=x_acc[:, i, :], in0=yg[:, b, :], scalar=wgt[:, k, i:i + 1],
                                           in1=x_acc[:, i, :], op0=ALU.mult,
                                           op1=ALU.add).then_inc((add1, add2)[k], 1)

            def add_shared(n):
                dve.wait_ge(down_ready, n + 1)
                dve.wait_ge(add2, 2 * n + 2)
                two = x_acc[:, 2 * n:2 * n + 2, :].rearrange("p a b -> p (a b)")
                g, h = n // 2, n % 2
                v.tensor_tensor(two, two, ps[:, 4 + 2 * (g % 2) + h, :], ALU.add).then_inc(fin_s, 1)

            for i in range(CHUNKS + 1):
                if i < CHUNKS:
                    s_hidden(i)
                if i >= 1:
                    s_low(i - 1)
                if i % 3 == 0 and i:
                    g = i // 3 - 1
                    for t in range(g * TG, (g + 1) * TG):
                        add_routed(t)
                if i % 3 == 1 and i > 3:
                    g = i // 3 - 1
                    add_shared(2 * g)
                    add_shared(2 * g + 1)
            add_shared(2 * NG - 2)
            add_shared(2 * NG - 1)

        @block.tensor
        def _(pe):
            t_ = nc.tensor

            def three(out_ap, ws_, xs_, start, stop):
                t_.matmul(out_ap, ws_[0], xs_[0], start=start, stop=False)
                t_.matmul(out_ap, ws_[0], xs_[1], start=False, stop=False)
                return t_.matmul(out_ap, ws_[1], xs_[0], start=False, stop=stop)

            def rows_to_columns(g):
                for k in range(KD):
                    if g >= 2:
                        pe.wait_ge(xT_lo_ready, 2 * (g - 2) + k + 1)
                    for i in range(TG):
                        if k == 0:
                            pe.wait_ge(xn_ready, g * TG + i + 1)
                        mm = t_.transpose(ps[:, 2 + 2 * (g % 2) + k, i * P:(i + 1) * P],
                                          xn_rows[:, (g * TG + i) % 8, k * P:(k + 1) * P], cst[:, C_ID:C_ID + P])
                    mm.then_inc(tr_ready, 1)

            def logits(g):
                pe.wait_ge(xT_lo_ready, 2 * g + 2)
                if g:
                    pe.wait_ge(lg_copied, g)
                cols = slice(g * GT, (g + 1) * GT)
                for k in range(KD):
                    e8 = slice(k * E, (k + 1) * E)
                    mm = three(ps[0:E, B_PROJ, :], (wr_hi[:, e8], wr_lo[:, e8]),
                               (xT_hi[:, k, cols], xT_lo[:, k, cols]), k == 0, k == KD - 1)
                mm.then_inc(lg_ready, 1)

            def logits_to_rows(g):
                pe.wait_ge(lg_copied, g + 1)
                for i in range(TG):
                    t = g * TG + i
                    mm = t_.transpose(ps[:, B_ROUTE, L_OFF + t * E:L_OFF + (t + 1) * E],
                                      lg[:, g % 2, i * P:(i + 1) * P], cst[0:E, C_ID:C_ID + E])
                mm.then_inc(logits_ready, 1)

            pe.wait_ge(cst_in, 16)
            rows_to_columns(0)
            rows_to_columns(1)
            pe.wait_ge(wr_lo_s, 1)
            logits(0)
            rows_to_columns(2)
            logits(1)
            logits_to_rows(0)
            rows_to_columns(3)
            logits(2)
            logits_to_rows(1)
            logits(3)
            logits_to_rows(2)
            logits_to_rows(3)

            def qkv(u):
                g, c, b = u // 2, u % 2, 3 * (u % 2)
                cols = slice(g * GT, (g + 1) * GT)
                for bank, part, read, done in ((B_K, 2, k_act, k_ready), (B_V, 4, kv_s, v_ready),
                                               (B_Q, 0, q_act, q_ready)):
                    if u >= 2:
                        pe.wait_ge(read, u - 1)
                    for k in range(KD):
                        w = slice(k * 3 * D + (part + c) * P, k * 3 * D + (part + c + 1) * P)
                        mm = three(ps[:, b + bank, :], (w_hi[:, w], w_lo[:, w]),
                                   (xT_hi[:, k, cols], xT_lo[:, k, cols]), k == 0, k == KD - 1)
                    mm.then_inc(done, 1)

            def project(n):
                g = n // 2
                pe.wait_ge(o_lo, 2 * g + 2)
                if n == 5:
                    pe.wait_ge(tok_ready, 1)
                elif n:
                    pe.wait_ge(acc_done, n - n // 6)
                for i in range(2):
                    cols = slice((2 * (n % 2) + i) * P, (2 * (n % 2) + i + 1) * P)
                    for c in range(KD):
                        s = (2 * g + c) % 4
                        w = slice(W_OUT + c * D, W_OUT + (c + 1) * D)
                        mm = three(ps[:, proj_bank(n), i * D:(i + 1) * D], (t_hi[:, s, cols], t_lo[:, s, cols]),
                                   (w_hi[:, w], w_lo[:, w]), c == 0, c == KD - 1)
                mm.then_inc(proj_ready, 1)

            def prefix():
                pe.wait_ge(mask_ready, 1)
                pe.wait_ge(ones_ready, 3)
                mask = rz[:].rearrange("p t e -> p (t e)")
                t_.matmul(ps[:, B_ROUTE, R_OFF:R_OFF + NT * E], cst[:, C_TRI:C_TRI + P], mask, start=True, stop=True)
                t_.matmul(ps[:, B_ROUTE, T_OFF:T_OFF + NT * E], ones[:], mask, start=True,
                          stop=True).then_inc(prefix_ready, 1)

            def table(k):
                hotp = xg[:].rearrange("p b d -> p (b d)").bitcast(F16).rearrange("p (i s) -> p i s", s=P)
                pe.wait_ge(hot_ready, k + 1)
                for i in range(NT):
                    mm = t_.matmul(ps[:, B_ROUTE, TAB_OFF:TAB_OFF + NS], hotp[:, i, :], hotj[:, k * NT + i, :],
                                   start=(k == 0 and i == 0), stop=(k == 1 and i == NT - 1))
                mm.then_inc(hot_used, 1)

            pe.wait_ge(wd_lo_s, 2)
            pe.wait_ge(xT_lo_ready, 2 * NG)
            for u in range(UNITS):
                qkv(u)
                if u == 2:
                    prefix()
                if u == 4:
                    table(0)
                if u == 5:
                    table(1)
                if u >= 4:
                    project(u - 4)

            def x_turn(t, b4, count):
                b = b4 % 2
                pe.wait_ge(gathered[b4], count)
                for k in range(KD):
                    mm = t_.transpose(ps[:, b, k * P:(k + 1) * P], xg[:, b4, k * P:(k + 1) * P],
                                      cst[:, C_ID:C_ID + P])
                mm.then_inc(xt_ready, 1)

            def gate_up(t, b, e):
                pe.wait_ge(xt_lo_s, t + 1)
                for k in range(KD):
                    w = bass.ds(e * EG + k * 2 * F, 2 * F)
                    xs = slice(b * D + k * P, b * D + (k + 1) * P)
                    mm = three(ps[:, 2 + b, 0:2 * F], (t_hi[:, 0, xs], t_lo[:, 0, xs]),
                               (eg_hi[:, w], eg_lo[:, w]), k == 0, k == KD - 1)
                mm.then_inc(gu_ready, 1)

            def h_turn(t, b):
                pe.wait_ge(h_s, t + 1)
                for k in range(2):
                    mm = t_.transpose(ps[0:FH, 4 + b, k * P:(k + 1) * P], h_buf[:, b, k * FH:(k + 1) * FH],
                                      cst[:, C_ID:C_ID + P])
                mm.then_inc(ht_ready, 1)

            def down(t, b, e):
                pe.wait_ge(ht_lo_s, t + 1)
                for k in range(2):
                    w = bass.ds(e * ED + k * D, D)
                    hs = slice(b * D + k * P, b * D + (k + 1) * P)
                    mm = three(ps[:, 6 + b, 0:D], (t_hi[0:FH, 1, hs], t_lo[0:FH, 1, hs]),
                               (ed_hi[:, w], ed_lo[:, w]), k == 0, k == 1)
                mm.then_inc(y_ready, 1)

            def experts_of(j, n=4):
                return nc.values_load_multi_w_load_instructions(
                    etab[0:1, bass.ds(j * 4, n + 2)], engines=[pe.engine], min_val=0, max_val=E - 1,
                    skip_runtime_bounds_check_because="a count of experts, capped at E - 1 when it was made")[1]

            def r_turn(j, n=4, first=False, last=False):
                e = experts_of(j, n)
                for b in range(n):
                    t = j * 4 + b
                    if not (last and b == n - 1):
                        x_turn(t + 1, (b + 1) % 4, (j + 1) * 16 if b < 3 else (j + 2) * 16)
                    gate_up(t, b % 2, e[b + 2])
                    if not (first and b == 0):
                        h_turn(t - 1, (b + 1) % 2)
                    if first and b == 1:
                        project(6)
                        project(7)
                        pe.wait_ge(acc_done, 8)
                    if not (first and b < 2):
                        down(t - 2, b % 2, e[b])
                return e[n:]

            pe.wait_ge(kv_s, UNITS)
            pe.wait_ge(q_act, UNITS)
            x_turn(0, 0, 16)
            project(4)
            project(5)
            pe.wait_ge(etab_ready, 1)
            pe.wait_ge(e_lo_s, 2 * E)
            r_turn(0, first=True)
            with pe.Fori(1, NS // 4) as j:
                r_turn(j)
            e_last = r_turn(NS // 4, n=NS % 4, last=True)
            h_turn(NS - 1, (NS - 1) % 2)
            down(NS - 2, (NS - 2) % 2, e_last[0])
            down(NS - 1, (NS - 1) % 2, e_last[1])

            def s_gate_up(i):
                g, (m0, n) = i // 3, SCH[i % 3]
                cols = slice(g * GT, (g + 1) * GT)
                for half, done in ((0, g_ready), (1, u_ready)):
                    if i >= 2:
                        pe.wait_ge((s_silu, s_h)[half], i - 1)
                    for k in range(KD):
                        w = slice(k * 2 * FS + half * FS + m0, k * 2 * FS + half * FS + m0 + n)
                        mm = three(ps[0:n, 2 * (i % 2) + half, :], (w_hi[:, w], w_lo[:, w]),
                                   (xT_hi[:, k, cols], xT_lo[:, k, cols]), k == 0, k == KD - 1)
                    mm.then_inc(done, 1)

            def s_down(g):
                pe.wait_ge(s_lo, 3 * g + 3)
                for h in range(2):
                    if g >= 2:
                        pe.wait_ge(fin_s, 2 * (g - 2) + h + 1)
                    for i in range(2):
                        cols = slice((2 * h + i) * P, (2 * h + i + 1) * P)
                        for m, (_, n) in enumerate(SCH):
                            s = (3 * g + m) % 4
                            w = slice(W_SDN + m * D, W_SDN + (m + 1) * D)
                            mm = three(ps[:, 4 + 2 * (g % 2) + h, i * D:(i + 1) * D],
                                       (t_hi[0:n, s, cols], t_lo[0:n, s, cols]),
                                       (w_hi[0:n, w], w_lo[0:n, w]), m == 0, m == 2)
                    mm.then_inc(down_ready, 1)

            pe.wait_ge(ws_lo_s, 3)
            pe.wait_ge(y_copied, NS)
            for i in range(CHUNKS):
                s_gate_up(i)
                if i % 3 == 0 and i:
                    s_down(i // 3 - 1)
            s_down(NG - 1)


def constants():
    import numpy as np
    c = np.zeros((P, C_END), np.float32)
    p = np.arange(P)
    c[:, C_ID:C_ID + P] = np.eye(P)
    c[:, C_TRI:C_TRI + P] = p[:, None] < p[None, :]
    c[:, C_DESC:C_DESC + E] = E - np.arange(E)
    c[:, C_RESET:C_RESET + E * NT] = (np.arange(E * NT) % NT) != 0
    c[:, C_THR:C_THR + NT] = P * np.arange(NT)
    c[:, C_I40:C_I40 + NS] = np.arange(NS)
    c[:, C_I128:C_I128 + P] = p
    c[:, C_TOK:C_TOK + 2 * NT] = p[:, None] + P * (np.arange(2 * NT) % NT)
    return c


def laid_out(a):
    import numpy as np

    def rows(w, k):
        return w.reshape(k, w.shape[0] // k, w.shape[1]).transpose(1, 0, 2).reshape(w.shape[0] // k, -1)

    gu = np.concatenate([a["L0_ffn_w_gate"], a["L0_ffn_w_up"]], axis=2)
    sgu = np.concatenate([a["L0_ffn_ws_gate"], a["L0_ffn_ws_up"]], axis=1)
    sdn = a["L0_ffn_ws_down"]
    return {
        "x": a["L0_attn_x"].reshape(T, D),
        "consts": constants(),
        "wr": rows(a["L0_ffn_w_router"], KD),
        "wqkv": rows(a["L0_attn_W_qkv"].T, KD),
        "wout": rows(a["L0_attn_W_out"].T, KD),
        "wsgu": rows(sgu, KD),
        "wsdn_a": rows(sdn[0:2 * P], 2),
        "wsdn_b": sdn[2 * P:],
        "egu": gu.reshape(E, KD, P, 2 * F).transpose(2, 0, 1, 3).reshape(P, E, EG),
        "edn": a["L0_ffn_w_down"].reshape(E, 2, FH, D).transpose(2, 0, 1, 3).reshape(FH, E, ED),
    }


def kernel(**inputs):
    import numpy as np
    import concourse.bacc as bacc
    from concourse.bass_utils import run_bass_kernel_spmd

    nc = bacc.Bacc("TRN2", target_bir_lowering=False, num_devices=1)
    arrays = {n: np.ascontiguousarray(v) for n, v in laid_out({k: np.asarray(v) for k, v in inputs.items()}).items()}
    args = [nc.dram_tensor(n, v.shape, F32, kind="ExternalInput").ap() for n, v in arrays.items()]
    out = nc.dram_tensor("out", (T, D), F32, kind="ExternalOutput").ap()
    build(nc, *args, out)
    r = run_bass_kernel_spmd(nc, [arrays], core_ids=[0])
    return r.results[0]["out"].reshape(4, T // 4, D)
```

```python
from contextlib import ExitStack

import concourse.bass as bass
from concourse import mybir

F32 = mybir.dt.float32
F32R = mybir.dt.float32r
F16 = mybir.dt.float16
I32 = mybir.dt.int32
ALU = mybir.AluOpType
ACT = mybir.ActivationFunctionType
AX = mybir.AxisListType.X

EARLY = 3
P = 128
T = 2048
D = 256
KD = D // P
NT = T // P
GT = 512
NG = T // GT
TG = GT // P
E = 8
F = 176
FB = F - P
FS = 352
SCH = [(0, 128), (128, 128), (256, 96)]
NS = 39
SCALE = 2.5
HD_SCALE = 0.25
EPS_LN = 1e-5
EPS_ATT = 1e-9

C_ID, C_TRI, C_DESC, C_RESET, C_FULL, C_TILE, C_SLOT, C_TOK, C_END = (
    0, 128, 256, 264, 392, 408, 448, 576, 608)

W_OUT = KD * 3 * D
W_SDN = KD * 2 * FS
W_COLS = W_SDN + 3 * D
EG = KD * 2 * F
ED = 2 * D

B_K, B_V, B_Q, B_PROJ, B_ROUTE = 0, 1, 2, 6, 7
L_OFF, R_OFF, T_OFF, TAB_OFF = 0, 128, 256, 384

W_EQ, W_EK, W_RQ, W_RK, W_NUM, W_P, W_KC, W_KVC, W_SLOTS = range(0, 18, 2)

UNITS = 2 * NG
CHUNKS = 3 * NG
WD = (0, W_OUT, W_OUT + KD * D)
WS = (0, W_SDN // 2, W_SDN, W_SDN + 2 * D, W_COLS)
WS_ROWS = (P, P, P, SCH[2][1])


def wait_if(eng, s, n):
    if not (isinstance(n, int) and n <= 0):
        eng.wait_ge(s, n)


def proj_bank(n):
    return {4: B_ROUTE, 5: B_V + 3, 6: B_ROUTE}.get(n, B_PROJ)


def build(nc, x, consts, wr, wqkv, wout, wsgu, wsdn_a, wsdn_b, egu, edn, out):
    xn_dram = nc.dram_tensor("xn_rows", (T, D), F32).ap()
    y_dram = nc.dram_tensor("y_rows", (NS * P, D), F32).ap()

    with ExitStack() as ctx:
        def sb(name, shape, dt):
            return ctx.enter_context(nc.sbuf_tensor(name, shape, dt))

        def sem(name):
            return ctx.enter_context(nc.semaphore(name))

        ps = ctx.enter_context(nc.psum_tensor("ps", [P, 8, 512], F32))
        x_acc = sb("x_acc", [P, NT, D], F32)
        xT_hi = sb("xT_hi", [P, KD, T], F32R)
        xT_lo = sb("xT_lo", [P, KD, T], F32R)
        w_hi = sb("w_hi", [P, W_COLS], F32R)
        w_lo = sb("w_lo", [P, W_COLS], F32R)
        wr_raw = sb("wr_raw", [P, KD * E], F32)
        wr_hi = sb("wr_hi", [P, KD * E], F32R)
        wr_lo = sb("wr_lo", [P, KD * E], F32R)
        eg_hi = sb("eg_hi", [P, E * EG], F32R)
        eg_lo = sb("eg_lo", [P, E * EG], F32R)
        ed_hi = sb("ed_hi", [P, E * ED], F32R)
        ed_lo = sb("ed_lo", [P, E * ED], F32R)
        e_raw = sb("e_raw", [P, EG + ED], F32)
        t_hi = sb("t_hi", [P, 4, GT], F32R)
        t_lo = sb("t_lo", [P, 4, GT], F32R)
        work = sb("work", [P, W_SLOTS, GT], F32)
        xg = sb("xg", [P, 4, D], F32)
        cst = sb("cst", [P, C_END], F32)
        ones = sb("ones", [P, P], F32)
        stats = sb("stats", [P, TG, 6], F32)
        mv = sb("mv", [P, NT, 2], F32)
        std = sb("std", [P, NT], F32)
        rz = sb("rz", [P, NT, E], F32)
        rp = sb("rp", [P, NT, E], F32)
        rc = sb("rc", [P, NT, E], F32)
        m1_mem = sb("m1", [P, NT * E], F32)
        m2 = sb("m2", [P, NT, E], F32)
        small = sb("small", [P, 8, NT], F32)
        wgt = sb("wgt", [P, 2, NT], F32)
        pm_i = sb("pm_i", [P, 2 * NT], I32)
        eps_col = sb("eps_col", [P, 1], F32)
        slot = sb("slot", [P, 2 * NT], F32)
        slot_i = sb("slot_i", [P, 2 * NT], I32)
        pm = sb("pm", [P, 2 * NT], F16)
        jm = sb("jm", [P, 2 * NT], F16)
        hot_mem = sb("hot_mem", [P, 2 * NT * NS], F16)
        tok_i = sb("tok_i", [P, NS], I32)
        etab_f = sb("etab_f", [1, NS], F32)
        etab = sb("etab", [1, NS + 2], I32)

        x_in = [sem(f"x_in{g}") for g in range(NG + 1)]
        cst_in, wr_in, wd_in, ws_in = (sem(n) for n in ("cst_in", "wr_in", "wd_in", "ws_in"))
        e_in = [sem(f"e_in{e}") for e in range(E)]
        xn_out, acc_out = sem("xn_out"), sem("acc_out")
        stat_s, var_ready, std_ready, rstd_ready, xn_ready = (
            sem(n) for n in ("stat_s", "var_ready", "std_ready", "rstd_ready", "xn_ready"))
        tr_ready, xT_hi_ready, xT_lo_ready, logits_ready = (
            sem(n) for n in ("tr_ready", "xT_hi_ready", "xT_lo_ready", "logits_ready"))
        ones_ready, wr_hi_s, wr_lo_s = sem("ones_ready"), sem("wr_hi_s"), sem("wr_lo_s")
        wd_hi_s, wd_lo_s, ws_hi_s, ws_lo_s, e_hi_s, e_lo_s = (
            sem(n) for n in ("wd_hi_s", "wd_lo_s", "ws_hi_s", "ws_lo_s", "e_hi_s", "e_lo_s"))
        k_ready, v_ready, q_ready, k_act, q_act = (
            sem(n) for n in ("k_ready", "v_ready", "q_ready", "k_act", "q_act"))
        phik_s, kv_s, kc_s, kvc_s, phiq_s = (sem(n) for n in ("phik_s", "kv_s", "kc_s", "kvc_s", "phiq_s"))
        den_s, num_s, ln_s, rec_s, out_s, o_hi, o_lo = (
            sem(n) for n in ("den_s", "num_s", "ln_s", "rec_s", "out_s", "o_hi", "o_lo"))
        proj_ready, acc_done = sem("proj_ready"), sem("acc_done")
        rt, z_ready, ez_ready, mask_ready, prefix_ready = (
            sem(n) for n in ("rt", "z_ready", "ez_ready", "mask_ready", "prefix_ready"))
        hot_ready, hot_used, tok_ready, etab_ready, slots_ready = (
            sem(n) for n in ("hot_ready", "hot_used", "tok_ready", "etab_ready", "slots_ready"))
        gathered = [sem(f"gathered{b}") for b in range(4)]
        xt_ready, xt_hi_s, xt_lo_s, gu_ready, silu_s, h_s = (
            sem(n) for n in ("xt_ready", "xt_hi_s", "xt_lo_s", "gu_ready", "silu_s", "h_s"))
        ht_ready, ht_hi_s, ht_lo_s, y_ready, y_copied = (
            sem(n) for n in ("ht_ready", "ht_hi_s", "ht_lo_s", "y_ready", "y_copied"))
        y_stored = [sem(f"y_stored{b}") for b in range(2)]
        g_ready, u_ready, s_silu, s_h, s_hi, s_lo, down_ready = (
            sem(n) for n in ("g_ready", "u_ready", "s_silu", "s_h", "s_hi", "s_lo", "down_ready"))
        y_in = [sem(f"y_in{b}") for b in range(8)]
        add1, add2, fin_s = sem("add1"), sem("add2"), sem("fin_s")
        lg_ready, lg_copied = sem("lg_ready"), sem("lg_copied")
        o_lo_last = sem("o_lo_last")
        pad_ready = sem("pad_ready")

        def flat(i, n=1):
            return work[:, i:i + n, :].rearrange("p a b -> p (a b)")

        ws_raw = flat(0, 5)[:, 0:W_COLS]
        xn_rows = flat(W_NUM, 4).rearrange("p (i d) -> p i d", d=D)

        m1 = m1_mem[:].rearrange("p (t e) -> p t e", e=E)
        c16 = m1_mem[:].bitcast(F16)[:, 0:C_END - C_TILE]
        hotj = hot_mem[:].rearrange("p (i n) -> p i n", n=NS)
        before_hot = hot_mem[:].bitcast(F32)
        tot = before_hot[:, 0:E * NT].rearrange("p (e t) -> p e t", e=E)
        etab_w = before_hot[0:1, E * NT:E * (NT + NS)].rearrange("p (j e) -> p j e", e=E)

        def raw_expert(e):
            if e % 2 == 0 or e == E - 1:
                return e_raw[:, 0:EG], e_raw[:, EG:EG + ED]
            return xg[:].rearrange("p b d -> p (b d)")[:, 0:EG], work[:, W_EQ + 1, :]

        wd_raw = flat(W_KC, 4)
        lg = work[0:E, W_RQ + 1:W_RK + 2:2, :]

        s_buf = work[:, W_KC, 0:2 * F].rearrange("p (b f) -> p b f", b=2)
        h_buf = work[:, W_KC + 1, :].rearrange("p (b f) -> p b f", b=2)
        y_buf = work[:, W_P, :].rearrange("p (b f) -> p b f", b=2)

        def xt(t, b):
            return t[:, 0, b * D:(b + 1) * D]

        def ht(t, b):
            return t[:, 1, b * D:(b + 1) * D]

        yg = flat(W_KC, 4).rearrange("p (b d) -> p b d", b=8)

        def s_ring(t, i):
            if i % 6 < 4:
                return t[:, i % 6, :]
            e = (eg_hi, eg_lo)[t is t_lo]
            return e[:, (i % 6 - 4) * GT:(i % 6 - 3) * GT]

        block = ctx.enter_context(nc.Block())

        @block.sync
        def _(sp):
            xv = x.rearrange("(t p) d -> p t d", p=P)
            ov = out.rearrange("(t p) d -> p t d", p=P)
            nv = xn_dram.rearrange("(t p) d -> p t d", p=P)
            yv = y_dram.rearrange("(t p) d -> p t d", p=P)

            for h in range(2):
                sp.dma_start(x_acc[:, 2 * h:2 * h + 2, :], xv[:, 2 * h:2 * h + 2, :]).then_inc(x_in[NG * h], 16)
            for g in range(1, NG):
                sp.dma_start(x_acc[:, g * TG:(g + 1) * TG, :],
                             xv[:, g * TG:(g + 1) * TG, :]).then_inc(x_in[g], 16)
                if g == 1:
                    sp.dma_start(cst[:], consts).then_inc(cst_in, 16)
                    sp.dma_start(wr_raw[:], wr).then_inc(wr_in, 16)
            sp.dma_start(wd_raw[:, 0:W_OUT], wqkv).then_inc(wd_in, 16)
            sp.dma_start(wd_raw[:, W_OUT:W_OUT + KD * D], wout).then_inc(wd_in, 16)

            def expert(e):
                if e >= 2:
                    before = e - 2 if e < E - 1 else e - 1
                    sp.wait_ge(e_hi_s, 2 * before + 2)
                    sp.wait_ge(e_lo_s, 2 * before + 2)
                g, d = raw_expert(e)
                sp.dma_start(g, egu[:, e, :]).then_inc(e_in[e], 16)
                sp.dma_start(d, edn[:, e, :]).then_inc(e_in[e], 16)

            for g in range(NG):
                sp.wait_ge(xn_ready, TG * (g + 1))
                sp.dma_start(nv[:, g * TG:(g + 1) * TG, :],
                             xn_rows[:, TG * (g % 2):TG * (g % 2 + 1), :]).then_inc(xn_out, 16)
                if g < 2:
                    expert(g)
                if g < NG - 1:
                    sp.wait_ge(xn_out, 16 * (g + 1))
            for e in range(2, E):
                expert(e)
            sp.wait_ge(o_lo, UNITS - 3)
            sp.wait_ge(o_lo_last, 3)
            sp.dma_start(ws_raw[:, 0:W_SDN], wsgu).then_inc(ws_in, 16)
            sp.dma_start(ws_raw[:, W_SDN:W_SDN + 2 * D], wsdn_a).then_inc(ws_in, 16)
            sp.dma_start(ws_raw[0:SCH[2][1], W_SDN + 2 * D:W_COLS], wsdn_b).then_inc(ws_in, 16)
            with sp.Fori(0, NS // 2) as j:
                for b in range(2):
                    sp.wait_ge(y_copied, j * 2 + (b + 1))
                    sp.dma_start(yv[:, bass.ds(j * 2 + b, 1), :],
                                 y_buf[:, b:b + 1, :]).then_inc(y_stored[b], 16)
            sp.wait_ge(y_copied, NS)
            sp.dma_start(yv[:, NS - 1:NS, :], y_buf[:, 0:1, :]).then_inc(y_stored[0], 16)
            for g in range(NG):
                for h in range(2):
                    sp.wait_ge(fin_s, 2 * g + h + 1)
                    a = TG * g + 2 * h
                    sp.dma_start(ov[:, a:a + 2, :], x_acc[:, a:a + 2, :]).then_inc(acc_out, 16)
            sp.wait_ge(acc_out, 16 * 2 * NG)
            sp.wait_ge(xn_out, 16 * NG)

        @block.gpsimd
        def _(pool):
            q = nc.gpsimd
            q.memset(ones[:], 1.0).then_inc(ones_ready, 1)
            q.memset(eps_col[:], EPS_ATT).then_inc(ones_ready, 1)
            q.memset(etab[:], 0).then_inc(ones_ready, 1)

            def low(dst, raw, high, done):
                q.tensor_tensor(dst, raw, high.bitcast(F32), ALU.subtract).then_inc(done, 1)

            pool.wait_ge(wr_hi_s, 1)
            low(wr_lo[:], wr_raw[:], wr_hi[:], wr_lo_s)

            def expert_low(u):
                pool.wait_ge(e_hi_s, 2 * u + 2)
                g, d = slice(u * EG, (u + 1) * EG), slice(u * ED, (u + 1) * ED)
                raw_g, raw_d = raw_expert(u)
                low(eg_lo[:, g], raw_g, eg_hi[:, g], e_lo_s)
                low(ed_lo[:, d], raw_d, ed_hi[:, d], e_lo_s)

            def gather(t):
                q.indirect_dma_start(
                    out=xg[:, t % 4, :], out_offset=None, in_=xn_dram,
                    in_offset=bass.IndirectOffsetOnAxis(ap=tok_i[:, t:t + 1], axis=0),
                ).then_inc(gathered[t % 4], 16)

            for h in range(2):
                pool.wait_ge(wd_hi_s, h + 1)
                low(w_lo[:, WD[h]:WD[h + 1]], wd_raw[:, WD[h]:WD[h + 1]], w_hi[:, WD[h]:WD[h + 1]], wd_lo_s)
            for e in range(EARLY):
                expert_low(e)

            def out_low(u):
                pool.wait_ge(o_hi, u + 1)
                low(t_lo[:, u % 4, :], work[:, W_NUM + u % 2, :], t_hi[:, u % 4, :], o_lo)

            for u in range(UNITS):
                c = u % 2
                if 2 <= u < UNITS - 1:
                    out_low(u - 2)
                if u == 0:
                    pool.wait_ge(xn_out, 16 * NG)
                if u == UNITS - 1:
                    gather(2)
                pool.wait_ge(phiq_s, u + 1)
                pool.wait_ge(kc_s, u + 1)
                if u >= 2:
                    pool.wait_ge(out_s, u - 1)
                q.tensor_tensor(work[:, W_P + c, :], work[:, W_RQ + c, :], work[:, W_KC + c, :],
                                ALU.mult).then_inc(den_s, 1)
                if u == UNITS - 2:
                    gather(1)
                if u == UNITS - 1:
                    break
                pool.wait_ge(kvc_s, u + 1)
                if u >= 2:
                    pool.wait_ge(o_lo, u - 1)
                q.tensor_tensor(work[:, W_NUM + c, :], work[:, W_RQ + c, :], work[:, W_KVC + c, :],
                                ALU.mult).then_inc(num_s, 1)
                if u + EARLY < E:
                    expert_low(u + EARLY)
                if u == UNITS - 3:
                    pool.wait_ge(tok_ready, 1)
                    gather(0)
            pool.wait_ge(den_s, UNITS)
            pad = h_buf.rearrange("p b (h f) -> p b h f", f=P // 2)[:, :, 2:4, FB:P // 2]
            q.memset(pad, 0.0).then_inc(pad_ready, 1)
            gather(3)

            def shared_low(h):
                n = WS_ROWS[h]
                pool.wait_ge(ws_hi_s, h + 1)
                low(w_lo[0:n, WS[h]:WS[h + 1]], ws_raw[0:n, WS[h]:WS[h + 1]], w_hi[0:n, WS[h]:WS[h + 1]], ws_lo_s)

            for t in range(4, NS):
                pool.wait_ge(xt_ready, t - 3)
                gather(t)
                if 8 <= t < 12:
                    shared_low(t - 8)

            for b in range(2):
                pool.wait_ge(y_stored[b], 16 * ((NS + 1 - b) // 2))
            for i in range(NT):
                for k in range(2):
                    b = (2 * i + k) % 8
                    if i >= 4:
                        pool.wait_ge((add1, add2)[k], i - 3)
                    q.indirect_dma_start(
                        out=yg[:, b, :], out_offset=None, in_=y_dram,
                        in_offset=bass.IndirectOffsetOnAxis(ap=slot_i[:, k * NT + i:k * NT + i + 1], axis=0),
                    ).then_inc(y_in[b], 16)

        @block.scalar
        def _(act):
            a = nc.scalar

            def high(dst, raw, done):
                a.activation(dst, raw, ACT.Copy).then_inc(done, 1)

            def sqrt(g):
                act.wait_ge(var_ready, g + 1)
                a.activation(std[:, g * TG:(g + 1) * TG], mv[:, g * TG:(g + 1) * TG, 1],
                             ACT.Sqrt).then_inc(std_ready, 1)

            def xT_high(g):
                for k in range(KD):
                    act.wait_ge(tr_ready, 2 * g + k + 1)
                    high(xT_hi[:, k, g * GT:(g + 1) * GT], ps[:, 3 + (2 * g + k) % 3, :], xT_hi_ready)

            def logits_copy(g):
                act.wait_ge(lg_ready, g + 1)
                if g >= 2:
                    act.wait_ge(logits_ready, g - 1)
                a.activation(lg[:, g % 2, :], ps[0:E, B_PROJ, :], ACT.Copy).then_inc(lg_copied, 1)

            def expert_high(e):
                g, d = slice(e * EG, (e + 1) * EG), slice(e * ED, (e + 1) * ED)
                act.wait_ge(e_in[e], 32)
                raw_g, raw_d = raw_expert(e)
                high(eg_hi[:, g], raw_g, e_hi_s)
                high(ed_hi[:, d], raw_d, e_hi_s)

            def k_parts(u):
                c, b = u % 2, 3 * (u % 2)
                act.wait_ge(k_ready, u + 1)
                if u >= 2:
                    act.wait_ge(kvc_s, u - 1)
                a.activation(work[:, W_EK + c, :], ps[:, b + B_K, :], ACT.Exp)
                a.activation(work[:, W_RK + c, :], ps[:, b + B_K, :], ACT.Relu).then_inc(k_act, 1)

            def q_parts(u):
                c, b = u % 2, 3 * (u % 2)
                act.wait_ge(q_ready, u + 1)
                if u >= 1:
                    act.wait_ge(phiq_s, u)
                if u >= 2:
                    act.wait_ge(num_s, u - 1)
                a.activation(work[:, W_EQ, :], ps[:, b + B_Q, :], ACT.Exp)
                a.activation(work[:, W_RQ + c, :], ps[:, b + B_Q, :], ACT.Relu).then_inc(q_act, 1)

            def dense_high(h):
                high(w_hi[:, WD[h]:WD[h + 1]], wd_raw[:, WD[h]:WD[h + 1]], wd_hi_s)

            sqrt(0)
            sqrt(1)
            act.wait_ge(wr_in, 16)
            high(wr_hi[:], wr_raw[:], wr_hi_s)
            xT_high(0)
            sqrt(2)
            act.wait_ge(wd_in, 32)
            dense_high(0)
            xT_high(1)
            dense_high(1)
            sqrt(3)
            a.preload_act_table_set("natural_log_exp_and_others")
            logits_copy(0)
            expert_high(0)
            xT_high(2)
            logits_copy(1)
            xT_high(3)
            k_parts(0)
            logits_copy(2)
            expert_high(1)

            def reciprocal(u):
                d = work[:, W_P + u % 2, :]
                act.wait_ge(den_s, u + 1)
                a.activation(d, d, ACT.Ln, bias=eps_col[:, 0:1]).then_inc(ln_s, 1)
                act.wait_ge(ln_s, u + 1)
                a.activation(d, d, ACT.Exp, scale=-1.0).then_inc(rec_s, 1)

            def out_high(u):
                act.wait_ge(out_s, u + 1)
                if u >= 4:
                    act.wait_ge(proj_ready, 2 * ((u - 4) // 2 + 1))
                high(t_hi[:, u % 4, :], work[:, W_NUM + u % 2, :], o_hi)

            act.wait_ge(ones_ready, 3)
            logits_copy(3)
            q_parts(0)
            act.wait_ge(z_ready, 1)
            a.activation(rz[:], rz[:], ACT.Exp).then_inc(ez_ready, 1)
            expert_high(2)
            for u in range(UNITS):
                if u >= 1:
                    k_parts(u)
                if u >= 2:
                    out_high(u - 2)
                if u >= 1:
                    q_parts(u)
                    reciprocal(u - 1)
                if u + EARLY < E:
                    expert_high(u + EARLY)

            def shared_high(h):
                n = WS_ROWS[h]
                high(w_hi[0:n, WS[h]:WS[h + 1]], ws_raw[0:n, WS[h]:WS[h + 1]], ws_hi_s)

            def h_high(t, b):
                act.wait_ge(ht_ready, t + 1)
                wait_if(act, y_ready, t - 1)
                high(ht(t_hi, b), ps[:, 4 + b, 0:D], ht_hi_s)

            def x_high(t, b):
                act.wait_ge(xt_ready, t + 1)
                wait_if(act, gu_ready, t - 1)
                high(xt(t_hi, b), ps[:, b, 0:D], xt_hi_s)

            def silu(t, b):
                act.wait_ge(gu_ready, t + 1)
                wait_if(act, h_s, t - 1)
                a.activation(s_buf[:, b, :], ps[:, 2 + b, 0:F], ACT.Silu).then_inc(silu_s, 1)

            def y_copy(t, b, stored):
                act.wait_ge(y_ready, t + 1)
                wait_if(act, y_stored[b], stored)
                a.activation(y_buf[:, b, :], ps[:, 6 + b, 0:D], ACT.Copy).then_inc(y_copied, 1)

            def r_step(j, b, first=False, behind=True, ahead=True):
                t = j * 2 + b
                if ahead:
                    x_high(t + 1, 1 - b)
                silu(t, b)
                if not first:
                    h_high(t - 1, 1 - b)
                if behind:
                    y_copy(t - 2, b, (j - 1) * 16)

            act.wait_ge(proj_ready, 6)
            x_high(0, 0)
            out_high(UNITS - 2)
            x_high(1, 1)
            reciprocal(UNITS - 1)
            a.preload_act_table(ACT.Silu)
            silu(0, 0)
            out_high(UNITS - 1)
            r_step(0, 1, behind=False)
            for h in range(4):
                r_step(1 + h // 2, h % 2)
                if h == 0:
                    act.wait_ge(ws_in, 48)
                    act.wait_ge(proj_ready, 2 * NG)
                shared_high(h)
            with act.Fori(3, NS // 2) as j:
                for b in range(2):
                    r_step(j, b)
            r_step(NS // 2, 0, ahead=False)
            h_high(NS - 1, 0)
            y_copy(NS - 2, 1, 16 * (NS // 2 - 1))

            def s_high(i):
                n = SCH[i % 3][1]
                act.wait_ge(s_h, i + 1)
                if i < 6:
                    act.wait_ge(y_ready, NS)
                else:
                    act.wait_ge(down_ready, 2 * ((i - 6) // 3 + 1))
                high(s_ring(t_hi, i)[0:n], work[0:n, 2 + i % 2, :], s_hi)

            act.wait_ge(ws_lo_s, 4)
            for i in range(CHUNKS):
                n = SCH[i % 3][1]
                act.wait_ge(g_ready, i + 1)
                if i >= 2:
                    act.wait_ge(s_h, i - 1)
                a.activation(work[0:n, i % 2, :], ps[0:n, 2 * (i % 2), :], ACT.Silu).then_inc(s_silu, 1)
                if i == 0:
                    y_copy(NS - 1, 0, 16 * (NS // 2))
                if i >= 1:
                    s_high(i - 1)
            s_high(CHUNKS - 1)

        @block.vector
        def _(dve):
            v = nc.vector

            def low(dst, full, high, done):
                v.tensor_tensor(dst, full, high.bitcast(F32), ALU.subtract).then_inc(done, 1)

            def row_stats(g):
                dve.wait_ge(x_in[g], 16)
                if g:
                    dve.wait_ge(stat_s, 8 * g)
                for i in range(TG):
                    if (g, i) == (0, 2):
                        dve.wait_ge(x_in[NG], 16)
                    v.bn_stats(stats[:, i, :], x_acc[:, g * TG + i, :]).then_inc(stat_s, 1)
                dve.wait_ge(stat_s, 8 * g + 4)
                for i in range(TG):
                    v.bn_aggr(mv[:, g * TG + i, :], stats[:, i, :]).then_inc(stat_s, 1)
                dve.wait_ge(stat_s, 8 * g + 8)
                var = mv[:, g * TG:(g + 1) * TG, 1]
                v.tensor_scalar(var, var, EPS_LN, None, ALU.add).then_inc(var_ready, 1)

            def normed(g):
                dve.wait_ge(std_ready, g + 1)
                r = std[:, g * TG:(g + 1) * TG]
                v.reciprocal(r, r).then_inc(rstd_ready, 1)
                dve.wait_ge(rstd_ready, g + 1)
                if g >= 2:
                    dve.wait_ge(xn_out, 16 * (g - 1))
                    dve.wait_ge(tr_ready, 2 * (g - 1))
                for i in range(g * TG, (g + 1) * TG):
                    v.tensor_scalar(xn_rows[:, i % 8, :], x_acc[:, i, :], mv[:, i, 0:1], std[:, i:i + 1],
                                    ALU.subtract, ALU.mult).then_inc(xn_ready, 1)

            def xT_low(g):
                for k in range(KD):
                    dve.wait_ge(xT_hi_ready, 2 * g + k + 1)
                    cols = slice(g * GT, (g + 1) * GT)
                    low(xT_lo[:, k, cols], ps[:, 3 + (2 * g + k) % 3, :], xT_hi[:, k, cols], xT_lo_ready)

            row_stats(0)
            row_stats(1)
            normed(0)
            row_stats(2)
            normed(1)
            xT_low(0)
            row_stats(3)
            normed(2)
            xT_low(1)
            normed(3)
            xT_low(2)
            xT_low(3)

            n_rt = [0]

            def link(ins, wait=True):
                n_rt[0] += 1
                ins.then_inc(rt, 1)
                if wait:
                    dve.wait_ge(rt, n_rt[0])

            def over_e(ap):
                return ap.unsqueeze(2).broadcast_to([P, NT, E])

            logits = ps[:, B_ROUTE, L_OFF:L_OFF + NT * E].rearrange("p (t e) -> p t e", e=E)
            desc = cst[:, C_DESC:C_DESC + E].unsqueeze(1).broadcast_to([P, NT, E])
            mx, sm, p1, p2, c1, ws = (small[:, n, :] for n in range(6))

            def route_logits():
                dve.wait_ge(logits_ready, NG)
                link(v.tensor_reduce(mx, logits, AX, ALU.max))
                v.tensor_tensor(rz[:], logits, over_e(mx), ALU.subtract).then_inc(z_ready, 1)

            def first_max(mask, top):
                link(v.tensor_reduce(top, rp[:], AX, ALU.max))
                link(v.tensor_tensor(rc[:], rp[:], over_e(top), ALU.is_equal))
                link(v.tensor_tensor(rc[:], rc[:], desc, ALU.mult))
                link(v.tensor_reduce(c1, rc[:], AX, ALU.max))
                link(v.tensor_tensor(mask, rc[:], over_e(c1), ALU.is_equal))

            def route_top2():
                dve.wait_ge(ez_ready, 1)
                link(v.tensor_reduce(sm, rz[:], AX, ALU.add))
                link(v.reciprocal(sm, sm))
                link(v.tensor_tensor(rp[:], rz[:], over_e(sm), ALU.mult))
                dve.wait_ge(cst_in, 16)
                first_max(m1[:], p1)
                link(v.scalar_tensor_tensor(out=rp[:], in0=m1[:], scalar=-2.0, in1=rp[:],
                                            op0=ALU.mult, op1=ALU.add))
                first_max(m2[:], p2)
                v.tensor_tensor(rz[:], m1[:], m2[:], ALU.add).then_inc(mask_ready, 1)

            def route_weights():
                link(v.tensor_tensor(ws, p1, p2, ALU.add))
                link(v.reciprocal(ws, ws))
                for k, pk in enumerate((p1, p2)):
                    link(v.scalar_tensor_tensor(out=wgt[:, k, :], in0=pk, scalar=SCALE, in1=ws,
                                                op0=ALU.mult, op1=ALU.mult))

            def route_slots():
                et = rc[:].rearrange("p t e -> p (t e)").rearrange("p (e t) -> p e t", e=E)
                cum = rp[:].rearrange("p t e -> p (t e)").rearrange("p (e t) -> p e t", e=E)
                one = ones[:, 0:E]
                dve.wait_ge(prefix_ready, 1)
                link(v.tensor_copy(et, ps[:, B_ROUTE, T_OFF:T_OFF + NT * E].rearrange("p (t e) -> p e t", e=E)))
                link(v.tensor_tensor_scan(rp[:].rearrange("p t e -> p (t e)"), cst[:, C_RESET:C_RESET + NT * E],
                                          rc[:].rearrange("p t e -> p (t e)"), 0.0, ALU.mult, ALU.add))
                thr = cst[:, C_FULL:C_FULL + NT].unsqueeze(1).broadcast_to([P, E, NT])
                link(v.tensor_tensor(tot[:, :, 0:NT], cum[:, :, NT - 1:NT].broadcast_to([P, E, NT]), thr, ALU.is_gt))
                link(v.tensor_reduce(small[:, 6, 0:E], tot[:, :, 0:NT], AX, ALU.add), wait=False)
                link(v.tensor_tensor(rp[:].rearrange("p t e -> p (t e)"), rp[:].rearrange("p t e -> p (t e)"),
                                     rc[:].rearrange("p t e -> p (t e)"), ALU.subtract))
                dve.wait_ge(ones_ready, 3)
                link(v.tensor_tensor_scan(small[:, 6, E:2 * E], one, small[:, 6, 0:E], 0.0, ALU.mult, ALU.add))
                link(v.tensor_tensor(small[:, 7, 0:E], small[:, 6, E:2 * E], small[:, 6, 0:E], ALU.subtract))
                link(v.tensor_scalar(small[:, 7, 0:E], small[:, 7, 0:E], float(P), None, ALU.mult))
                link(v.tensor_tensor(cum, cum, small[:, 7, 0:E].unsqueeze(2).broadcast_to([P, E, NT]), ALU.add))
                before = ps[:, B_ROUTE, R_OFF:R_OFF + NT * E].rearrange("p (t e) -> p t e", e=E)
                link(v.tensor_tensor(rc[:], before, cum.rearrange("p e t -> p t e"), ALU.add))
                for k, m in enumerate((m1, m2)):
                    link(v.tensor_tensor(m[:], m[:], rc[:], ALU.mult), wait=k == 1)
                for k, m in enumerate((m1, m2)):
                    link(v.tensor_reduce(slot[:, k * NT:(k + 1) * NT], m[:], AX, ALU.add), wait=k == 1)
                v.tensor_copy(slot_i[:], slot[:]).then_inc(slots_ready, 1)
                dve.wait_ge(slots_ready, 1)
                link(v.tensor_scalar(pm_i[:], slot_i[:], P - 1, None, ALU.bitwise_and), wait=False)
                tile_no = cst[0:1, C_TILE:C_TILE + NS].unsqueeze(2).broadcast_to([1, NS, E])
                ends = small[0:1, 6, E:2 * E].unsqueeze(1).broadcast_to([1, NS, E])
                link(v.tensor_tensor(etab_w[:], tile_no, ends, ALU.is_ge))
                link(v.tensor_copy(pm[:], pm_i[:]), wait=False)
                link(v.tensor_reduce(etab_f[:], etab_w[:], AX, ALU.add))
                link(v.tensor_tensor(jm[:], slot[:], pm[:], ALU.subtract))
                link(v.tensor_scalar(jm[:], jm[:], 1.0 / P, None, ALU.mult), wait=False)
                v.tensor_scalar(etab[:, 2:NS + 2], etab_f[:], float(E - 1), None, ALU.min).then_inc(etab_ready, 1)

            hotp = xg[:].rearrange("p b d -> p (b d)").bitcast(F16).rearrange("p (i s) -> p i s", s=P)

            def route_hot(k):
                if k == 0:
                    link(v.tensor_copy(c16, cst[:, C_TILE:C_END]))
                    dve.wait_ge(e_lo_s, 2 * (E - 2))
                    tile_no = c16[:, 0:NS].unsqueeze(1).broadcast_to([P, 2 * NT, NS])
                    link(v.tensor_tensor(hotj[:], jm[:].unsqueeze(2).broadcast_to([P, 2 * NT, NS]), tile_no, ALU.is_equal))
                    tok = c16[:, C_TOK - C_TILE:C_TOK - C_TILE + 2 * NT].unsqueeze(2).broadcast_to([P, 2 * NT, NS])
                    link(v.tensor_tensor(hotj[:], hotj[:], tok, ALU.mult))
                else:
                    dve.wait_ge(hot_used, 1)
                slot_no = c16[:, C_SLOT - C_TILE:C_SLOT - C_TILE + P].unsqueeze(1).broadcast_to([P, NT, P])
                v.tensor_tensor(hotp, pm[:, k * NT:(k + 1) * NT].unsqueeze(2).broadcast_to([P, NT, P]), slot_no,
                                ALU.is_equal).then_inc(hot_ready, 1)

            def route_table():
                dve.wait_ge(hot_used, 2)
                v.tensor_copy(tok_i[:], ps[:, B_ROUTE, TAB_OFF:TAB_OFF + NS]).then_inc(tok_ready, 1)

            def keys(u):
                c, b = u % 2, 3 * (u % 2)
                ek, rk = work[:, W_EK + c, :], work[:, W_RK + c, :]
                dve.wait_ge(k_act, u + 1)
                v.scalar_tensor_tensor(out=rk, in0=ek, scalar=1.0, in1=rk, op0=ALU.min,
                                       op1=ALU.add).then_inc(phik_s, 1)
                dve.wait_ge(phik_s, u + 1)
                dve.wait_ge(v_ready, u + 1)
                v.tensor_tensor(ek, rk, ps[:, b + B_V, :], ALU.mult).then_inc(kv_s, 1)

            def sums(u):
                c = u % 2
                ek, rk = work[:, W_EK + c, :], work[:, W_RK + c, :]
                kc, kvc = work[:, W_KC + c, :], work[:, W_KVC + c, :]
                dve.wait_ge(phik_s, u + 1)
                if u >= 2:
                    dve.wait_ge(den_s, u - 1)
                else:
                    dve.wait_ge(wd_lo_s, 2)
                one = ones[:, 0:1].broadcast_to([P, GT])
                v.tensor_tensor_scan(kc, one, rk, 0.0, ALU.mult,
                                     ALU.add).then_inc(kc_s, 1)
                dve.wait_ge(kv_s, u + 1)
                if u >= 2:
                    dve.wait_ge(num_s, u - 1)
                v.tensor_tensor_scan(kvc, one, ek, 0.0, ALU.mult,
                                     ALU.add).then_inc(kvc_s, 1)

            def queries(u):
                c = u % 2
                rq = work[:, W_RQ + c, :]
                dve.wait_ge(q_act, u + 1)
                v.scalar_tensor_tensor(out=rq, in0=work[:, W_EQ, :], scalar=1.0, in1=rq, op0=ALU.min,
                                       op1=ALU.add).then_inc(phiq_s, 1)

            def divided(u):
                n = work[:, W_NUM + u % 2, :]
                dve.wait_ge(rec_s, u + 1)
                dve.wait_ge(num_s, u + 1)
                v.tensor_tensor(n, n, work[:, W_P + u % 2, :], ALU.mult).then_inc(out_s, 1)

            def out_low(u):
                dve.wait_ge(o_hi, u + 1)
                low(t_lo[:, u % 4, :], work[:, W_NUM + u % 2, :], t_hi[:, u % 4, :], o_lo_last)

            def add_proj(n):
                dve.wait_ge(proj_ready, n + 1)
                two = x_acc[:, 2 * n:2 * n + 2, :].rearrange("p a b -> p (a b)")
                v.scalar_tensor_tensor(out=two, in0=ps[:, proj_bank(n), :], scalar=HD_SCALE, in1=two, op0=ALU.mult,
                                       op1=ALU.add).then_inc(acc_done, 1)

            dve.wait_ge(ones_ready, 3)
            keys(0)
            sums(0)
            route_logits()
            queries(0)
            for u in range(UNITS):
                if u >= 1:
                    keys(u)
                    if u == UNITS - 1:
                        out_low(u - 2)
                    sums(u)
                if u >= 4:
                    add_proj(u - 4)
                if u >= 1:
                    queries(u)
                    divided(u - 1)
                if u == UNITS - 1:
                    dve.wait_ge(phiq_s, UNITS)
                    dve.wait_ge(kvc_s, UNITS)
                    dve.wait_ge(o_lo_last, 1)
                    v.tensor_tensor(work[:, W_NUM + 1, :], work[:, W_RQ + 1, :], work[:, W_KVC + 1, :],
                                    ALU.mult).then_inc(num_s, 1)
                if u == 0:
                    route_top2()
                if u == 2:
                    route_slots()
                if u == 3:
                    route_hot(0)
                if u == 4:
                    route_hot(1)
                if u == 5:
                    route_table()

            def h_low(t, b):
                dve.wait_ge(ht_hi_s, t + 1)
                v.tensor_tensor(ht(t_lo, b)[:, 0:P], ps[:, 4 + b, 0:P], ht(t_hi, b)[:, 0:P].bitcast(F32), ALU.subtract)
                second = ht(t_hi, b)[P // 2:P, P:2 * P]
                low(second, ps[P // 2:P, 4 + b, P:2 * P], second, ht_lo_s)

            def x_low(t, b):
                dve.wait_ge(xt_hi_s, t + 1)
                low(xt(t_lo, b), ps[:, b, 0:D], xt(t_hi, b), xt_lo_s)

            def hidden(t, b):
                dve.wait_ge(silu_s, t + 1)
                wait_if(dve, ht_ready, t - 1)
                v.tensor_tensor(h_buf[:, b, 0:F], s_buf[:, b, :], ps[:, 2 + b, F:2 * F], ALU.mult)
                v.tensor_tensor(h_buf[:, b, D - P // 2:D - P // 2 + FB], s_buf[:, b, P:F], ps[:, 2 + b, F + P:2 * F],
                                ALU.mult).then_inc(h_s, 1)

            def r_step(j, b, first=False, behind=True, ahead=True):
                t = j * 2 + b
                if ahead:
                    x_low(t + 1, 1 - b)
                hidden(t, b)
                if not first:
                    h_low(t - 1, 1 - b)

            x_low(0, 0)
            add_proj(4)
            add_proj(5)
            out_low(UNITS - 2)
            x_low(1, 1)
            divided(UNITS - 1)
            dve.wait_ge(pad_ready, 1)
            hidden(0, 0)
            out_low(UNITS - 1)
            r_step(0, 1, behind=False)
            for n in range(6, 8):
                add_proj(n)
            route_weights()
            with dve.Fori(1, NS // 2) as j:
                for b in range(2):
                    r_step(j, b)
            r_step(NS // 2, 0, ahead=False)
            h_low(NS - 1, 0)

            def s_hidden(i):
                n = SCH[i % 3][1]
                dve.wait_ge(s_silu, i + 1)
                dve.wait_ge(u_ready, i + 1)
                if i >= 2:
                    dve.wait_ge(s_lo, i - 1)
                v.tensor_tensor(work[0:n, 2 + i % 2, :], work[0:n, i % 2, :], ps[0:n, 2 * (i % 2) + 1, :],
                                ALU.mult).then_inc(s_h, 1)

            def s_low(i):
                n = SCH[i % 3][1]
                dve.wait_ge(s_hi, i + 1)
                low(s_ring(t_lo, i)[0:n], work[0:n, 2 + i % 2, :], s_ring(t_hi, i)[0:n], s_lo)

            def add_routed(i):
                for k in range(2):
                    b = (2 * i + k) % 8
                    dve.wait_ge(y_in[b], 16 * (i // 4 + 1))
                    if k:
                        dve.wait_ge(add1, i + 1)
                    v.scalar_tensor_tensor(out=x_acc[:, i, :], in0=yg[:, b, :], scalar=wgt[:, k, i:i + 1],
                                           in1=x_acc[:, i, :], op0=ALU.mult,
                                           op1=ALU.add).then_inc((add1, add2)[k], 1)

            def add_shared(n):
                dve.wait_ge(down_ready, n + 1)
                dve.wait_ge(add2, 2 * n + 2)
                two = x_acc[:, 2 * n:2 * n + 2, :].rearrange("p a b -> p (a b)")
                g, h = n // 2, n % 2
                v.tensor_tensor(two, two, ps[:, 4 + 2 * (g % 2) + h, :], ALU.add).then_inc(fin_s, 1)

            ADDED = (0, 0, 0, 1, 3, 5, 7, 9, 11, 12, 13, 13)
            for i in range(CHUNKS):
                s_hidden(i)
                if i >= 1:
                    s_low(i - 1)
                for t in range(ADDED[i - 1] if i else 0, ADDED[i]):
                    add_routed(t)
                if i in (5, 9):
                    add_shared(i // 2 - 2)
                    add_shared(i // 2 - 1)
            s_low(CHUNKS - 1)
            add_shared(2 * NG - 4)
            add_routed(NT - 3)
            add_shared(2 * NG - 3)
            add_routed(NT - 2)
            add_routed(NT - 1)
            add_shared(2 * NG - 2)
            add_shared(2 * NG - 1)

        @block.tensor
        def _(pe):
            t_ = nc.tensor

            def three(out_ap, ws_, xs_, start, stop):
                t_.matmul(out_ap, ws_[0], xs_[0], start=start, stop=False)
                t_.matmul(out_ap, ws_[0], xs_[1], start=False, stop=False)
                return t_.matmul(out_ap, ws_[1], xs_[0], start=False, stop=stop)

            def rows_to_columns(g):
                for k in range(KD):
                    if 2 * g + k >= 3:
                        pe.wait_ge(xT_lo_ready, 2 * g + k - 2)
                    for i in range(TG):
                        if k == 0:
                            pe.wait_ge(xn_ready, g * TG + i + 1)
                        mm = t_.transpose(ps[:, 3 + (2 * g + k) % 3, i * P:(i + 1) * P],
                                          xn_rows[:, (g * TG + i) % 8, k * P:(k + 1) * P], cst[:, C_ID:C_ID + P])
                    mm.then_inc(tr_ready, 1)

            def logits(g):
                pe.wait_ge(xT_lo_ready, 2 * g + 2)
                if g:
                    pe.wait_ge(lg_copied, g)
                cols = slice(g * GT, (g + 1) * GT)
                for k in range(KD):
                    e8 = slice(k * E, (k + 1) * E)
                    mm = three(ps[0:E, B_PROJ, :], (wr_hi[:, e8], wr_lo[:, e8]),
                               (xT_hi[:, k, cols], xT_lo[:, k, cols]), k == 0, k == KD - 1)
                mm.then_inc(lg_ready, 1)

            def logits_to_rows(g):
                pe.wait_ge(lg_copied, g + 1)
                for i in range(TG):
                    t = g * TG + i
                    mm = t_.transpose(ps[:, B_ROUTE, L_OFF + t * E:L_OFF + (t + 1) * E],
                                      lg[:, g % 2, i * P:(i + 1) * P], cst[0:E, C_ID:C_ID + E])
                mm.then_inc(logits_ready, 1)

            def qkv(u, parts=("k", "v", "q")):
                g, c, b = u // 2, u % 2, 3 * (u % 2)
                cols = slice(g * GT, (g + 1) * GT)
                for name in parts:
                    bank, part, read, done = {"k": (B_K, 2, k_act, k_ready), "v": (B_V, 4, kv_s, v_ready),
                                              "q": (B_Q, 0, q_act, q_ready)}[name]
                    if u >= 2:
                        pe.wait_ge(read, u - 1)
                    for k in range(KD):
                        w = slice(k * 3 * D + (part + c) * P, k * 3 * D + (part + c + 1) * P)
                        mm = three(ps[:, b + bank, :], (w_hi[:, w], w_lo[:, w]),
                                   (xT_hi[:, k, cols], xT_lo[:, k, cols]), k == 0, k == KD - 1)
                    mm.then_inc(done, 1)

            def project(n):
                g = n // 2
                pe.wait_ge(o_lo, min(2 * g + 2, UNITS - 3))
                if g >= 2:
                    pe.wait_ge(o_lo_last, 2 * g - 3)
                pe.wait_ge(wd_lo_s, 2)
                if n == 4:
                    pe.wait_ge(tok_ready, 1)
                elif n == 5:
                    pe.wait_ge(kv_s, UNITS)
                elif n:
                    pe.wait_ge(acc_done, {6: 5, 7: 4}.get(n, n))
                for i in range(2):
                    cols = slice((2 * (n % 2) + i) * P, (2 * (n % 2) + i + 1) * P)
                    for c in range(KD):
                        s = (2 * g + c) % 4
                        w = slice(W_OUT + c * D, W_OUT + (c + 1) * D)
                        mm = three(ps[:, proj_bank(n), i * D:(i + 1) * D], (t_hi[:, s, cols], t_lo[:, s, cols]),
                                   (w_hi[:, w], w_lo[:, w]), c == 0, c == KD - 1)
                mm.then_inc(proj_ready, 1)

            def prefix():
                pe.wait_ge(mask_ready, 1)
                pe.wait_ge(ones_ready, 3)
                mask = rz[:].rearrange("p t e -> p (t e)")
                t_.matmul(ps[:, B_ROUTE, R_OFF:R_OFF + NT * E], cst[:, C_TRI:C_TRI + P], mask, start=True, stop=True)
                t_.matmul(ps[:, B_ROUTE, T_OFF:T_OFF + NT * E], ones[:], mask, start=True,
                          stop=True).then_inc(prefix_ready, 1)

            def table(k):
                hotp = xg[:].rearrange("p b d -> p (b d)").bitcast(F16).rearrange("p (i s) -> p i s", s=P)
                pe.wait_ge(hot_ready, k + 1)
                for i in range(NT):
                    mm = t_.matmul(ps[:, B_ROUTE, TAB_OFF:TAB_OFF + NS], hotp[:, i, :], hotj[:, k * NT + i, :],
                                   start=(k == 0 and i == 0), stop=(k == 1 and i == NT - 1))
                mm.then_inc(hot_used, 1)

            pe.wait_ge(cst_in, 16)
            rows_to_columns(0)
            rows_to_columns(1)
            pe.wait_ge(wr_lo_s, 1)
            logits(0)
            rows_to_columns(2)
            logits(1)
            logits_to_rows(0)
            rows_to_columns(3)
            pe.wait_ge(wd_lo_s, 1)
            qkv(0, ("k",))
            logits(2)
            logits_to_rows(1)
            qkv(0, ("v",))
            logits(3)
            logits_to_rows(2)
            qkv(0, ("q",))
            logits_to_rows(3)
            for u in range(UNITS):
                if u == 1:
                    pe.wait_ge(xT_lo_ready, 2 * NG)
                if u:
                    qkv(u)
                if u == 2:
                    prefix()
                if u == 5:
                    table(0)
                if u == 6:
                    table(1)
                if u >= 4:
                    project(u - 4)

            def x_turn(t, b4, count):
                b = b4 % 2
                pe.wait_ge(gathered[b4], count)
                for k in range(KD):
                    mm = t_.transpose(ps[:, b, k * P:(k + 1) * P], xg[:, b4, k * P:(k + 1) * P],
                                      cst[:, C_ID:C_ID + P])
                mm.then_inc(xt_ready, 1)

            def gate_up(t, b, e):
                pe.wait_ge(xt_lo_s, t + 1)
                for k in range(KD):
                    w = bass.ds(e * EG + k * 2 * F, 2 * F)
                    xs = slice(b * D + k * P, b * D + (k + 1) * P)
                    mm = three(ps[:, 2 + b, 0:2 * F], (t_hi[:, 0, xs], t_lo[:, 0, xs]),
                               (eg_hi[:, w], eg_lo[:, w]), k == 0, k == KD - 1)
                mm.then_inc(gu_ready, 1)

            def h_turn(t, b):
                pe.wait_ge(h_s, t + 1)
                for k in range(2):
                    cols = slice(k * P, (k + 1) * P)
                    mm = t_.transpose(ps[:, 4 + b, cols], h_buf[:, b, cols], cst[:, C_ID:C_ID + P])
                mm.then_inc(ht_ready, 1)

            def down(t, b, e):
                pe.wait_ge(ht_lo_s, t + 1)
                w, w2 = bass.ds(e * ED, D), bass.ds(e * ED + D, D)
                y, first, second = ps[:, 6 + b, 0:D], slice(b * D, b * D + P), slice(b * D + P, (b + 1) * D)
                three(y, (t_hi[:, 1, first], t_lo[:, 1, first]), (ed_hi[:, w], ed_lo[:, w]), True, False)
                t_.matmul(y, t_hi[:, 1, second], ed_hi[:, w2], start=False, stop=False)
                t_.matmul(y, t_hi[0:P // 2, 1, second], ed_lo[0:P // 2, w2], start=False,
                          stop=True).then_inc(y_ready, 1)

            TURN = 8

            def experts_of(j, n=TURN):
                return nc.values_load_multi_w_load_instructions(
                    etab[0:1, bass.ds(j * TURN, n + 2)], engines=[pe.engine], min_val=0, max_val=E - 1,
                    skip_runtime_bounds_check_because="a count of experts, capped at E - 1 when it was made")[1]

            def r_turn(j, e, n=TURN, first=False, last=False):
                for b in range(n):
                    t = j * TURN + b
                    if not (last and b == n - 1):
                        x_turn(t + 1, (b + 1) % 4, j * (TURN // 4 * 16) + ((b + 1) // 4 + 1) * 16)
                    gate_up(t, b % 2, e[b + 2])
                    if not (first and b == 0):
                        h_turn(t - 1, (b + 1) % 2)
                    if first and b == 1:
                        project(6)
                        project(7)
                    if first and b == 2:
                        pe.wait_ge(acc_done, 8)
                    if not (first and b < 2):
                        down(t - 2, b % 2, e[b])
                return e[n:]

            pe.wait_ge(kv_s, UNITS - 1)
            x_turn(0, 0, 16)
            pe.wait_ge(etab_ready, 1)
            e_first = experts_of(0)
            project(4)
            project(5)
            pe.wait_ge(kv_s, UNITS)
            pe.wait_ge(q_act, UNITS)
            pe.wait_ge(e_lo_s, 2 * E)
            r_turn(0, e_first, first=True)
            with pe.Fori(1, NS // TURN) as j:
                r_turn(j, experts_of(j))
            e_last = r_turn(NS // TURN, experts_of(NS // TURN, NS % TURN), n=NS % TURN, last=True)

            def s_gate_up(i, halves=(0, 1)):
                g, (m0, n) = i // 3, SCH[i % 3]
                cols = slice(g * GT, (g + 1) * GT)
                for half in halves:
                    if i >= 2:
                        pe.wait_ge((s_silu, s_h)[half], i - 1)
                    for k in range(KD):
                        w = slice(k * 2 * FS + half * FS + m0, k * 2 * FS + half * FS + m0 + n)
                        mm = three(ps[0:n, 2 * (i % 2) + half, :], (w_hi[:, w], w_lo[:, w]),
                                   (xT_hi[:, k, cols], xT_lo[:, k, cols]), k == 0, k == KD - 1)
                    mm.then_inc((g_ready, u_ready)[half], 1)

            def s_down(g):
                pe.wait_ge(s_lo, 3 * g + 3)
                for h in range(2):
                    if g >= 2:
                        pe.wait_ge(fin_s, 2 * (g - 2) + h + 1)
                    for i in range(2):
                        cols = slice((2 * h + i) * P, (2 * h + i + 1) * P)
                        for m, (_, n) in enumerate(SCH):
                            w = slice(W_SDN + m * D, W_SDN + (m + 1) * D)
                            mm = three(ps[:, 4 + 2 * (g % 2) + h, i * D:(i + 1) * D],
                                       (s_ring(t_hi, 3 * g + m)[0:n, cols], s_ring(t_lo, 3 * g + m)[0:n, cols]),
                                       (w_hi[0:n, w], w_lo[0:n, w]), m == 0, m == 2)
                    mm.then_inc(down_ready, 1)

            pe.wait_ge(ws_lo_s, 4)
            s_gate_up(0, (0,))
            down(NS - 2, (NS - 2) % 2, e_last[0])
            h_turn(NS - 1, (NS - 1) % 2)
            s_gate_up(0, (1,))
            down(NS - 1, (NS - 1) % 2, e_last[1])
            for i in range(1, CHUNKS):
                s_gate_up(i)
                if i == 4:
                    pe.wait_ge(y_copied, NS)
                    s_down(0)
                if i == 8:
                    s_down(1)
            s_down(NG - 2)
            s_down(NG - 1)


def constants():
    import numpy as np
    c = np.zeros((P, C_END), np.float32)
    p = np.arange(P)
    c[:, C_ID:C_ID + P] = np.eye(P)
    c[:, C_TRI:C_TRI + P] = p[:, None] < p[None, :]
    c[:, C_DESC:C_DESC + E] = E - np.arange(E)
    c[:, C_RESET:C_RESET + E * NT] = (np.arange(E * NT) % NT) != 0
    c[:, C_FULL:C_FULL + NT] = P * np.arange(NT)
    c[:, C_TILE:C_TILE + NS] = np.arange(NS)
    c[:, C_SLOT:C_SLOT + P] = p
    c[:, C_TOK:C_TOK + 2 * NT] = p[:, None] + P * (np.arange(2 * NT) % NT)
    return c


def laid_out(a):
    import numpy as np

    def rows(w, k):
        return w.reshape(k, w.shape[0] // k, w.shape[1]).transpose(1, 0, 2).reshape(w.shape[0] // k, -1)

    gu = np.concatenate([a["L0_ffn_w_gate"], a["L0_ffn_w_up"]], axis=2)
    sgu = np.concatenate([a["L0_ffn_ws_gate"], a["L0_ffn_ws_up"]], axis=1)
    sdn = a["L0_ffn_ws_down"]
    down = np.zeros((E, 2, P, D), np.float32)
    down[:, 0] = a["L0_ffn_w_down"][:, 0:P]
    for h in range(2):
        down[:, 1, h * P // 2:h * P // 2 + FB] = a["L0_ffn_w_down"][:, P:]
    return {
        "x": a["L0_attn_x"].reshape(T, D),
        "consts": constants(),
        "wr": rows(a["L0_ffn_w_router"], KD),
        "wqkv": rows(a["L0_attn_W_qkv"].T, KD),
        "wout": rows(a["L0_attn_W_out"].T, KD),
        "wsgu": rows(sgu, KD),
        "wsdn_a": rows(sdn[0:2 * P], 2),
        "wsdn_b": sdn[2 * P:],
        "egu": gu.reshape(E, KD, P, 2 * F).transpose(2, 0, 1, 3).reshape(P, E, EG),
        "edn": down.transpose(2, 0, 1, 3).reshape(P, E, ED),
    }


def kernel(**inputs):
    import numpy as np
    import concourse.bacc as bacc
    from concourse.bass_utils import run_bass_kernel_spmd

    nc = bacc.Bacc("TRN2", target_bir_lowering=False, num_devices=1)
    arrays = {n: np.ascontiguousarray(v) for n, v in laid_out({k: np.asarray(v) for k, v in inputs.items()}).items()}
    args = [nc.dram_tensor(n, v.shape, F32, kind="ExternalInput").ap() for n, v in arrays.items()]
    out = nc.dram_tensor("out", (T, D), F32, kind="ExternalOutput").ap()
    build(nc, *args, out)
    r = run_bass_kernel_spmd(nc, [arrays], core_ids=[0])
    return r.results[0]["out"].reshape(4, T // 4, D)
```
